# Optimizing a Trainium2 kernel written in Bass

```python
import numpy as np
import jax
import jax.numpy as jnp

def _softmax(x, axis=-1):
    return jax.nn.softmax(x, axis=axis)

def _gelu(x):
    return jax.nn.gelu(x, approximate=True)

def _silu(x):
    return jax.nn.silu(x)

def _sigmoid(x):
    return jax.nn.sigmoid(x)

def _layernorm(x, axis=-1, eps=1e-05):
    m = jnp.mean(x, axis=axis, keepdims=True)
    v = jnp.var(x, axis=axis, keepdims=True)
    return (x - m) / jnp.sqrt(v + eps)

def _scatter_add(tgt, idx, src, axis=0):
    return tgt.at[idx].add(src)

def _segment_sum(src, seg, n):
    return jax.ops.segment_sum(src, seg, n)
kernel_name = 'mk_vit_tower_postln_d1_tok_img1024_r4_734a75'

def setup_inputs(seed: int=0):
    np.random.seed(seed)
    _w = jnp.asarray

    def _rec_inputs():
        import jax
        import jax.numpy as jnp
        _rk = jax.random.key(seed)
        x = -0.00016672 + 0.999947 * jax.random.normal(jax.random.fold_in(_rk, 1), (32, 3, 96, 96), jnp.float32)
        return x
    x = _rec_inputs()

    def _L0_tok_setup():
        import jax, jax.numpy as jnp
        import numpy as np
        EMBED_DIM = 256
        IMAGE_SIZE = 96
        CHANNELS = 3
        PATCH = 16
        NUM_PATCHES = (IMAGE_SIZE // PATCH) ** 2
        PATCH_DIM = PATCH * PATCH * CHANNELS

        def _patchify(x, patch):
            B, C, H, W = x.shape
            hp, wp = (H // patch, W // patch)
            x = x.reshape(B, C, hp, patch, wp, patch)
            x = x.transpose(0, 2, 4, 1, 3, 5)
            return x.reshape(B, hp * wp, C * patch * patch)
        key = jax.random.key(seed)
        k_x, k_w, k_b, k_cls, k_pos = jax.random.split(key, 5)
        x = jax.random.normal(k_x, (64, CHANNELS, IMAGE_SIZE, IMAGE_SIZE), dtype=jnp.float32)
        W = jax.random.normal(k_w, (EMBED_DIM, PATCH_DIM), dtype=jnp.float32) / np.sqrt(PATCH_DIM)
        b = jax.random.normal(k_b, (EMBED_DIM,), dtype=jnp.float32) * 0.01
        cls_token = jax.random.normal(k_cls, (1, 1, EMBED_DIM), dtype=jnp.float32)
        pos_embedding = jax.random.normal(k_pos, (1, 1 + NUM_PATCHES, EMBED_DIM), dtype=jnp.float32)
        return {'x': x, 'W': W, 'b': b, 'cls_token': cls_token, 'pos_embedding': pos_embedding}
    _L0_tok_all = _L0_tok_setup()
    _L0_tok_in = {k: v for k, v in _L0_tok_all.items() if k in ('W', 'b', 'cls_token', 'pos_embedding')}
    del _L0_tok_all

    def _L0_attn_setup():
        import jax, jax.numpy as jnp
        import numpy as np
        B, T, D_MODEL = (2, 256, 256)
        H, DEPTH = (8, 5)
        DH = D_MODEL // H
        key = jax.random.key(seed)
        k_x, k_wp, k_bp, k_wv, k_wo = jax.random.split(key, 5)
        x = jax.random.normal(k_x, (B, T, D_MODEL), dtype=jnp.float32)
        Wp = jax.random.normal(k_wp, (D_MODEL, H * DEPTH), dtype=jnp.float32) * 0.02
        bp = jnp.zeros((H * DEPTH,), dtype=jnp.float32)
        Wv = jax.random.normal(k_wv, (D_MODEL, D_MODEL), dtype=jnp.float32) * 0.02
        Wo = jax.random.normal(k_wo, (D_MODEL, D_MODEL), dtype=jnp.float32) * 0.02
        return {'x': x, 'Wp': Wp, 'bp': bp, 'Wv': Wv, 'Wo': Wo}
    _L0_attn_all = _L0_attn_setup()
    _L0_attn_in = {k: v for k, v in _L0_attn_all.items() if k in ('Wp', 'bp', 'Wv', 'Wo')}
    del _L0_attn_all

    def _L0_ffn_setup():
        import jax, jax.numpy as jnp
        import numpy as np
        B, S, H, F, G = (8, 512, 256, 1024, 128)
        EPS = 1e-05

        def _dequant(q, scales, g):
            K, N = q.shape
            w = (q.astype(jnp.float32) - 128.0).reshape(K // g, g, N) * scales[:, None, :]
            return w.reshape(K, N)
        key = jax.random.key(seed)
        ks = jax.random.split(key, 8)
        x = jax.random.normal(ks[0], (B, S, H), dtype=jnp.float32)
        ln_gamma = jnp.ones((H,), jnp.float32)
        ln_beta = jnp.zeros((H,), jnp.float32)
        fc1_q = jax.random.randint(ks[1], (H, F), 0, 64, dtype=jnp.int32)
        fc2_q = jax.random.randint(ks[2], (F, H), 0, 64, dtype=jnp.int32)
        fc1_scales = jax.random.uniform(ks[3], (H // G, F), jnp.float32) * 0.02 + 0.001
        fc2_scales = jax.random.uniform(ks[4], (F // G, H), jnp.float32) * 0.02 + 0.001
        fc1_bias = jax.random.normal(ks[5], (F,), jnp.float32) * 0.02
        fc2_bias = jax.random.normal(ks[6], (H,), jnp.float32) * 0.02
        return {'x': x, 'ln_gamma': ln_gamma, 'ln_beta': ln_beta, 'fc1_q': fc1_q, 'fc1_scales': fc1_scales, 'fc1_bias': fc1_bias, 'fc2_q': fc2_q, 'fc2_scales': fc2_scales, 'fc2_bias': fc2_bias}
    _L0_ffn_all = _L0_ffn_setup()
    _L0_ffn_in = {k: v for k, v in _L0_ffn_all.items() if k in ('ln_gamma', 'ln_beta', 'fc1_q', 'fc1_scales', 'fc1_bias', 'fc2_q', 'fc2_scales', 'fc2_bias')}
    del _L0_ffn_all
    return {'x': x, 'L0_tok_W': _L0_tok_in['W'], 'L0_tok_b': _L0_tok_in['b'], 'L0_tok_cls_token': _L0_tok_in['cls_token'], 'L0_tok_pos_embedding': _L0_tok_in['pos_embedding'], 'L0_attn_Wp': _L0_attn_in['Wp'], 'L0_attn_bp': _L0_attn_in['bp'], 'L0_attn_Wv': _L0_attn_in['Wv'], 'L0_attn_Wo': _L0_attn_in['Wo'], 'L0_ffn_ln_gamma': _L0_ffn_in['ln_gamma'], 'L0_ffn_ln_beta': _L0_ffn_in['ln_beta'], 'L0_ffn_fc1_q': _L0_ffn_in['fc1_q'], 'L0_ffn_fc1_scales': _L0_ffn_in['fc1_scales'], 'L0_ffn_fc1_bias': _L0_ffn_in['fc1_bias'], 'L0_ffn_fc2_q': _L0_ffn_in['fc2_q'], 'L0_ffn_fc2_scales': _L0_ffn_in['fc2_scales'], 'L0_ffn_fc2_bias': _L0_ffn_in['fc2_bias']}

def reference(x, L0_tok_W, L0_tok_b, L0_tok_cls_token, L0_tok_pos_embedding, L0_attn_Wp, L0_attn_bp, L0_attn_Wv, L0_attn_Wo, L0_ffn_ln_gamma, L0_ffn_ln_beta, L0_ffn_fc1_q, L0_ffn_fc1_scales, L0_ffn_fc1_bias, L0_ffn_fc2_q, L0_ffn_fc2_scales, L0_ffn_fc2_bias):
    import jax
    import jax.numpy as jnp

    def _L0_tok_ref(x, W, b, cls_token, pos_embedding):
        import jax, jax.numpy as jnp
        import numpy as np
        EMBED_DIM = 256
        IMAGE_SIZE = 96
        CHANNELS = 3
        PATCH = 16
        NUM_PATCHES = (IMAGE_SIZE // PATCH) ** 2
        PATCH_DIM = PATCH * PATCH * CHANNELS

        def _patchify(x, patch):
            B, C, H, W = x.shape
            hp, wp = (H // patch, W // patch)
            x = x.reshape(B, C, hp, patch, wp, patch)
            x = x.transpose(0, 2, 4, 1, 3, 5)
            return x.reshape(B, hp * wp, C * patch * patch)
        B = x.shape[0]
        patches = _patchify(x, PATCH)
        tokens = jnp.einsum('bnd,ed->bne', patches, W) + b
        cls = jnp.broadcast_to(cls_token, (B, 1, EMBED_DIM))
        out = jnp.concatenate([cls, tokens], axis=1)
        return out + pos_embedding

    def _L0_attn_ref(x, Wp, bp, Wv, Wo):
        import jax, jax.numpy as jnp
        import numpy as np
        B, T, D_MODEL = (2, 256, 256)
        H, DEPTH = (8, 5)
        DH = D_MODEL // H
        Bx, Tx, d = x.shape
        paths = jax.nn.sigmoid(x @ Wp + bp)
        paths = paths.reshape(Bx, Tx, H, DEPTH).transpose(0, 2, 1, 3)
        pq = paths[:, :, :, None, :]
        pk = paths[:, :, None, :, :]
        agree = pq * pk + (1.0 - pq) * (1.0 - pk)
        sim = jnp.cumprod(agree, axis=-1).sum(axis=-1) / DEPTH
        mask = jnp.triu(jnp.ones((Tx, Tx), dtype=bool), k=1)
        sim = jnp.where(mask[None, None], -jnp.inf, sim)
        attn = jax.nn.softmax(sim, axis=-1)
        V = (x @ Wv).reshape(Bx, Tx, H, DH).transpose(0, 2, 1, 3)
        ctx = jnp.einsum('bhqk,bhkd->bhqd', attn, V)
        ctx = ctx.transpose(0, 2, 1, 3).reshape(Bx, Tx, d)
        return ctx @ Wo

    def _L0_ffn_ref(x, ln_gamma, ln_beta, fc1_q, fc1_scales, fc1_bias, fc2_q, fc2_scales, fc2_bias):
        import jax, jax.numpy as jnp
        import numpy as np
        B, S, H, F, G = (8, 512, 256, 1024, 128)
        EPS = 1e-05

        def _dequant(q, scales, g):
            K, N = q.shape
            w = (q.astype(jnp.float32) - 128.0).reshape(K // g, g, N) * scales[:, None, :]
            return w.reshape(K, N)
        residual = x
        mu = jnp.mean(x, axis=-1, keepdims=True)
        var = jnp.mean(jnp.square(x - mu), axis=-1, keepdims=True)
        h = (x - mu) * jax.lax.rsqrt(var + EPS) * ln_gamma + ln_beta
        hf = h.reshape(-1, H)
        w1 = _dequant(fc1_q, fc1_scales, G)
        y = hf @ w1 + fc1_bias
        y = jax.nn.silu(y)
        w2 = _dequant(fc2_q, fc2_scales, G)
        z = y @ w2 + fc2_bias
        return residual + 0.5 * z.reshape(residual.shape)
    h = _L0_tok_ref(x, L0_tok_W, L0_tok_b, L0_tok_cls_token, L0_tok_pos_embedding)
    h = _layernorm(h + _L0_attn_ref(h, L0_attn_Wp, L0_attn_bp, L0_attn_Wv, L0_attn_Wo), axis=-1)
    h = _layernorm(h + _L0_ffn_ref(h, L0_ffn_ln_gamma, L0_ffn_ln_beta, L0_ffn_fc1_q, L0_ffn_fc1_scales, L0_ffn_fc1_bias, L0_ffn_fc2_q, L0_ffn_fc2_scales, L0_ffn_fc2_bias), axis=-1)
    return h

_drawn_inputs = setup_inputs


def setup_inputs(seed=0):
    import zlib

    import numpy as np

    out = dict(_drawn_inputs(seed))
    spreads = {'L0_attn_bp': (0.0, 2.0), 'L0_ffn_ln_gamma': (1.0, 0.2), 'L0_ffn_ln_beta': (0.0, 0.1)}
    factors = {'L0_tok_b': 30.648,
     'L0_tok_cls_token': 3.083,
     'L0_attn_Wp': 200.0,
     'L0_attn_Wo': 3.078,
     'L0_ffn_fc1_bias': 52.094,
     'L0_ffn_fc2_bias': 200.0}
    for name, (base, spread) in spreads.items():
        noise = np.random.default_rng([zlib.crc32(name.encode()), seed]).standard_normal(out[name].shape)
        drawn = base * np.exp(spread * noise) if base else spread * noise
        out[name] = jnp.asarray(drawn.astype(out[name].dtype))
    for name, factor in factors.items():
        out[name] = (out[name] * factor).astype(out[name].dtype)
    return out
```

```python
from contextlib import ExitStack

import concourse.bass as bass
from concourse import mybir

ALU = mybir.AluOpType
ACT = mybir.ActivationFunctionType
F32 = mybir.dt.float32
BF16 = mybir.dt.bfloat16
I32 = mybir.dt.int32
EPS = 1e-5
MASKED = -1e4
ZERO_POINT = 128.0


def vit_block(nc, x, tok_W, tok_b, cls_token, pos, Wp, bp, Wv, Wo, ln_gamma, ln_beta,
              fc1_q, fc1_scales, fc1_bias, fc2_q, fc2_scales, fc2_bias, out):
    B, C, IMG, _ = x.shape
    D, PATCH_DIM = tok_W.shape
    T = pos.shape[1]
    NP = T - 1
    PATCH = 16
    GRID = IMG // PATCH
    KT = PATCH_DIM // 128
    E2 = D // 128
    HALF = B // 2
    HR = HALF * GRID
    HD = Wp.shape[1]
    H = 8
    DEPTH = HD // H
    DH = D // H
    NTOK = B * T
    IT = 3
    R = IT * T
    TILES = -(-B // IT)
    CI = 8
    CHUNKS = B // CI
    CP, CT = CI * NP, CI * T
    F = fc1_q.shape[1]
    FB = F // 128
    FQ = FB // 2
    G1, G2 = fc1_scales.shape[0], fc2_scales.shape[0]
    BR = HD // 4
    UROWS = HD * T
    PARTS = 3
    HALF_AT = 64

    def images(t):
        return min(IT, B - t * IT) if isinstance(t, int) else IT

    def rows(t):
        return images(t) * T

    def there(t):
        return not isinstance(t, int) or 0 <= t < TILES

    def counts(n):
        return not isinstance(n, int) or n > 0

    with ExitStack() as ctx:
        def sb(name, shape, dt=F32):
            return ctx.enter_context(nc.sbuf_tensor(name, shape, dt))

        def ps(name, shape):
            return ctx.enter_context(nc.psum_tensor(name, shape, F32))

        def sem(name):
            return ctx.enter_context(nc.semaphore(name))

        bank_bc = ps("bank_bc", [128, 2, 512])
        bank_cd = ps("bank_cd", [128, 2, 512])
        bank_ctx, bank_turn = bank_cd[:, 0, :], bank_cd[:, 1, :]
        bank_y = ps("bank_y", [128, 512])
        bank_z = ps("bank_z", [128, 512])
        bank_v = ps("bank_v", [128, 512])
        bank_o = ps("bank_o", [128, 512])

        ident = sb("ident", [128, 128])
        x_rows_all = sb("x_rows", [128, 2 * C * PATCH * IMG])
        x_rows = x_rows_all[0:HR, :].rearrange("p (n k) -> p n k", n=2 * C)
        xT = sb("xT", [128, KT, B * NP])
        w_rows = sb("w_rows", [128, E2, PATCH_DIM])
        wT = sb("wT", [128, KT, D])
        pos_rows = sb("pos_rows", [T, D])
        N_VEC = 4 * E2
        vec_rows = sb("vec_rows", [N_VEC, 128])
        vec_cols = sb("vec_cols", [128, N_VEC])
        tokb_col, cls_col, gamma_col, beta_col = (vec_cols[:, i * E2:(i + 1) * E2] for i in range(4))
        posb = sb("posb", [128, E2, T])
        hT = sb("hT", [128, E2, NTOK])
        hT_proj = sb("hT_proj", [128, E2, R])
        hT_res = sb("hT_res", [128, E2, R])
        wvp = sb("wvp", [128, E2, D + HD])
        wp_dh = sb("wp_dh", [128, E2, HD])
        bp_half = sb("bp_half", [HD, 1])
        bp_row = sb("bp_row", [1, HD])
        bp_row_dh = sb("bp_row_dh", [1, HD])
        ones_row = sb("ones_row", [1, 128])
        path_f = sb("path_f", [HD, CT])
        path_rest = sb("path_rest", [HD, CT])
        path_parts = sb("path_parts", [HD, 2, PARTS, CT], BF16)
        q_parts = sb("q_parts", [128, UROWS], BF16)
        pick = sb("pick", [128, NTOK], BF16)
        path_k = sb("path_k", [128, HD])
        agree = sb("agree", [128, HD, T])
        causal = sb("causal", [128, T])
        own_image = sb("own_image", [128, IT])
        horner = sb("horner", [128, 2, H * T])
        sim = sb("sim", [128, H, T])
        probs = sb("probs", [128, H, IT, T])
        v_ones = sb("v_ones", [128, H, DH + 1])
        recip = sb("recip", [128, H])
        ctx_rows = sb("ctx_rows", [128, D])
        ctxT = sb("ctxT", [128, E2, R])
        wo = sb("wo", [128, E2, D])
        stats = sb("stats", [128, 6])
        mv = sb("mv", [128, 2])
        small = sb("small", [128, 4])
        rstd = sb("rstd", [128, 2])
        minus_half = sb("minus_half", [128, 1])
        eps_col = sb("eps_col", [128, 1])
        assert TILES * D <= 2 * PATCH * IMG
        patches = sb("patches", [128, 2 * PATCH * IMG])
        x_pat = patches[0:HR, :].rearrange("p (n g k) -> p n g k", n=2, g=GRID)
        h2 = patches[:, 0:TILES * D].rearrange("p (t d) -> p t d", t=TILES)
        n2 = sb("n2", [128, D])
        hnT = sb("hnT", [128, E2, NTOK])
        q1 = sb("q1", [128, G1, F], I32)
        q2 = sb("q2", [128, G2, D], I32)
        s1 = sb("s1", [128, G1, F])
        s2 = sb("s2", [128, G2, D])
        w1 = sb("w1", [128, G1, F])
        w2 = sb("w2", [128, G2, D])
        BIAS = 32 * PARTS
        bias_f = x_rows_all[0:BIAS, 0:F + D]
        bias_rest = x_rows_all[0:BIAS, F + D:2 * (F + D)]
        bias_mid = sb("bias_mid", [BIAS, F + D], BF16)
        bias_parts = sb("bias_parts", [BIAS, F + D], BF16)
        ones_bf = sb("ones_bf", [BIAS, 128], BF16)
        half_bf = sb("half_bf", [BIAS, 128], BF16)
        th = sb("th", [128, 2, FQ, R])
        act2 = sb("act2", [128, FB, R])
        res = sb("res", [128, D])
        fstats = sb("fstats", [128, 6])
        fmv = sb("fmv", [128, 2])
        fvar = sb("fvar", [128, 1])
        frstd = sb("frstd", [128, 1])
        fin = sb("fin", [128, D])

        path_dram = nc.dram_tensor("path_dram", (2, PARTS, HALF, HD, T), BF16, kind="Internal").ap()

        w_in = sem("w_in")
        x_in = [sem(f"x_in{i}") for i in range(2 * C)]
        par_in = sem("par_in")
        mats_in = sem("mats_in")
        q_in = sem("q_in")
        bias_in = sem("bias_in")
        consts = sem("consts")
        bias_step = sem("bias_step")
        colwise = sem("colwise")
        wT_psum = sem("wT_psum")
        wT_ready = sem("wT_ready")
        pos_psum = sem("pos_psum")
        posb_step = sem("posb_step")
        x_pat_ready = sem("x_pat_ready")
        xT_psum = sem("xT_psum")
        xT_dve = sem("xT_dve")
        xT_act = sem("xT_act")
        tok_psum = sem("tok_psum")
        hT_ready = sem("hT_ready")
        cls_ready = sem("cls_ready")
        path_psum = sem("path_psum")
        path_f_ready = sem("path_f_ready")
        path_hi_ready = sem("path_hi_ready")
        split_step = sem("split_step")
        path_out = sem("path_out")
        q_parts_in = sem("q_parts_in")
        s2_ready = sem("s2_ready")
        dequant = sem("dequant")
        hT_proj_in = sem("hT_proj_in")
        hT_res_in = sem("hT_res_in")
        proj_done = sem("proj_done")
        bcA_done = sem("bcA_done")
        bcB_done = sem("bcB_done")
        path_k_ready = sem("path_k_ready")
        v_ready = sem("v_ready")
        uA_done = sem("uA_done")
        uB_done = sem("uB_done")
        gA_done = sem("gA_done")
        gB_done = sem("gB_done")
        g0_done = sem("g0_done")
        horner_step = sem("horner_step")
        sim_ready = sem("sim_ready")
        probs_ready = sem("probs_ready")
        pv_done = sem("pv_done")
        recip_done = sem("recip_done")
        ctx_ready = sem("ctx_ready")
        ctxT_psum = sem("ctxT_psum")
        ctxT_ready = sem("ctxT_ready")
        wo_done = sem("wo_done")
        mv_ready = sem("mv_ready")
        rstd_step = sem("rstd_step")
        rstd_ready = sem("rstd_ready")
        h2_ready = sem("h2_ready")
        n2_ready = sem("n2_ready")
        n2T_psum = sem("n2T_psum")
        hnT_ready = sem("hnT_ready")
        y_psum = sem("y_psum")
        th_ready = sem("th_ready")
        act_ready = sem("act_ready")
        z_psum = sem("z_psum")
        res_ready = sem("res_ready")
        fmv_ready = sem("fmv_ready")
        frstd_step = sem("frstd_step")
        frstd_ready = sem("frstd_ready")
        fin_ready = sem("fin_ready")
        stored = sem("stored")

        N_CONST = 21
        N_PAR, N_MATS, N_Q = 7, 2, 4
        LOOP = range(4, TILES - 2)
        out_flat = out.rearrange("b t d -> (b t) d")


        def image_rows(ap, n):
            return ap.rearrange("p (b t) -> p b t", t=n)

        def spread(ap, n):
            return ap.rearrange("p (o t) -> p o t", o=1).broadcast_to([ap.shape[0], n, ap.shape[1]])

        block = ctx.enter_context(nc.Block())

        @block.sync
        def _(sp):
            sp.dma_start(w_rows[:], tok_W.rearrange("(e p) k -> p e k", p=128)).then_inc(w_in, 16)
            for half in range(2):
                for c in range(C):
                    n = half * C + c
                    src = x[half * HALF:(half + 1) * HALF, c].rearrange("b (g i) w -> b g (i w)", i=PATCH)
                    sp.dma_start(x_rows[:, n, :], src).then_inc(x_in[n], 16)
            sp.dma_start(wvp[:, :, 0:D], Wv.rearrange("(e p) n -> p e n", p=128)).then_inc(mats_in, 16)
            sp.dma_start(wo[:], Wo.rearrange("(e p) n -> p e n", p=128)).then_inc(mats_in, 16)

            def paths_out(c):
                half, first = divmod(c * CI, HALF)
                for part in range(PARTS):
                    if part == 0:
                        sp.wait_ge(path_hi_ready, c + 1)
                    else:
                        sp.wait_ge(split_step, 3 * c + part + 1)
                    sp.dma_start(path_dram[half, part, first:first + CI].rearrange("b r t -> r b t"),
                                 image_rows(path_parts[:, c % 2, part, :], T)).then_inc(path_out, 16)

            def paths_in(half):
                sp.wait_ge(path_out, 16 * PARTS * (half + 1) * CHUNKS // 2)
                sp.dma_start(q_parts[half * HALF_AT:half * HALF_AT + PARTS * HALF, :],
                             path_dram[half].rearrange("n b r t -> (n b) (r t)")).then_inc(q_parts_in, 16)

            def load_proj(t):
                if counts(t):
                    sp.wait_ge(proj_done, t)
                sp.dma_start(hT_proj[:, :, 0:rows(t)],
                             hT[:, :, bass.ds(t * R, rows(t))]).then_inc(hT_proj_in, 16)

            def load_res(t):
                if counts(t):
                    sp.wait_ge(wo_done, t)
                sp.dma_start(hT_res[:, :, 0:rows(t)],
                             hT[:, :, bass.ds(t * R, rows(t))]).then_inc(hT_res_in, 16)

            def store(t):
                n = rows(t)
                sp.wait_ge(fin_ready, t + 1)
                sp.dma_start(out_flat[bass.ds(t * R, n), :], fin[0:n, :]).then_inc(stored, 16)

            def slot(t):
                if there(t + 2):
                    load_proj(t + 2)
                if there(t):
                    load_res(t)
                if there(t - 4):
                    store(t - 4)

            sp.wait_ge(hT_ready, E2)
            sp.wait_ge(cls_ready, E2)
            load_proj(0)
            load_res(0)
            sp.wait_ge(consts, N_CONST)
            paths_out(0)
            paths_out(1)
            paths_in(0)
            load_proj(1)
            sp.dma_start(q1[:], fc1_q.rearrange("(g p) n -> p g n", p=128)).then_inc(q_in, 16)
            sp.dma_start(s1[:], fc1_scales.rearrange("(o g) n -> o g n", o=1).broadcast_to([128, G1, F])).then_inc(q_in, 16)
            sp.dma_start(q2[:], fc2_q.rearrange("(g p) n -> p g n", p=128)).then_inc(q_in, 16)
            sp.dma_start(s2[:], fc2_scales.rearrange("(o g) n -> o g n", o=1).broadcast_to([128, G2, D])).then_inc(q_in, 16)
            sp.wait_ge(bias_step, 1)
            for part in range(PARTS):
                p = 32 * part
                sp.dma_start(bias_f[p:p + 1, 0:F], fc1_bias.rearrange("(o n) -> o n", o=1)).then_inc(bias_in, 16)
                sp.dma_start(bias_f[p:p + 1, F:F + D], fc2_bias.rearrange("(o n) -> o n", o=1)).then_inc(bias_in, 16)
            paths_out(2)
            sp.wait_ge(hT_ready, E2 * CHUNKS // 2)
            load_proj(2)
            paths_out(3)
            paths_in(1)
            sp.wait_ge(hT_ready, E2 * CHUNKS)
            for t in range(1, LOOP.start):
                slot(t)
            with sp.Fori(LOOP.start, LOOP.stop - 1) as t:
                slot(t)
            for t in range(LOOP.stop - 1, TILES + 4):
                slot(t)
            sp.wait_ge(stored, 16 * TILES)

        @block.gpsimd
        def _(pool):
            def const(ins):
                ins.then_inc(consts, 1)

            const(pool.memset(ident[:], 1.0))
            pool.wait_ge(consts, 1)
            const(pool.affine_select(out=ident[:], in_=ident[:], compare_op=ALU.is_equal, fill=0.0, base=0,
                                     pattern=[[-1, 128]], channel_multiplier=1))
            const(pool.memset(q_parts[:], 0.0))
            const(pool.memset(pick[:], 0.0))
            pool.wait_ge(consts, 4)
            for part in range(PARTS):
                for half in range(2):
                    some = image_rows(pick[half * HALF_AT:(half + 1) * HALF_AT, half * HALF * T:(half + 1) * HALF * T], T)
                    const(pool.affine_select(out=some, in_=some, compare_op=ALU.not_equal, fill=1.0,
                                             base=part * HALF, pattern=[[1, HALF], [0, T]], channel_multiplier=-1))
                pool.wait_ge(consts, 6 + 2 * part)
            const(pool.memset(minus_half[:], -0.5))
            const(pool.memset(eps_col[:], EPS))
            const(pool.memset(ones_row[:], 1.0))
            const(pool.memset(v_ones[:], 1.0))
            const(pool.memset(own_image[:], 0.0))
            pool.wait_ge(consts, 15)
            const(pool.affine_select(out=own_image[:], in_=own_image[:], compare_op=ALU.is_ge, fill=MASKED, base=0,
                                     pattern=[[-T, IT]], channel_multiplier=1))
            pool.wait_ge(consts, 16)
            const(pool.affine_select(out=own_image[:], in_=own_image[:], compare_op=ALU.is_ge, fill=MASKED,
                                     base=T - 1, pattern=[[T, IT]], channel_multiplier=-1))
            const(pool.memset(causal[:], 0.5))
            pool.wait_ge(consts, 18)
            for b in reversed(range(IT)):
                const(pool.affine_select(out=causal[0:T * (b + 1)], in_=causal[0:T * (b + 1)], compare_op=ALU.is_ge,
                                         fill=MASKED, base=T * b, pattern=[[1, T]], channel_multiplier=-1))
                pool.wait_ge(consts, 18 + IT - b)

            def bias_step_done(ins):
                ins.then_inc(bias_step, 1)

            pool.wait_ge(x_pat_ready, 2 * C)
            bias_step_done(pool.memset(bias_f, 0.0))
            bias_step_done(pool.memset(ones_bf[:], 1.0))
            bias_step_done(pool.memset(half_bf[:], 0.5))

            def bias_split():
                pool.wait_ge(bias_in, 2 * PARTS * 16)
                bias_step_done(pool.tensor_copy(bias_parts[:], bias_f))
                pool.wait_ge(bias_step, 4)
                bias_step_done(pool.tensor_tensor(bias_rest, bias_f, bias_parts[:], ALU.subtract))
                pool.wait_ge(bias_step, 5)
                bias_step_done(pool.tensor_copy(bias_mid[:], bias_rest))
                pool.wait_ge(bias_step, 6)
                bias_step_done(pool.tensor_copy(bias_parts[32:64], bias_mid[32:64]))
                pool.wait_ge(bias_step, 7)
                bias_step_done(pool.tensor_tensor(bias_parts[64:96], bias_rest[64:96], bias_mid[64:96], ALU.subtract))
                pool.wait_ge(bias_step, 8)

            def last_agreement(t):
                n = rows(t)
                pool.wait_ge(uB_done, t + 1)
                pool.tensor_tensor(agree[0:n, 4 * H:5 * H, :], agree[0:n, 4 * H:5 * H, :],
                                   spread(causal[0:n, :], H), ALU.add).then_inc(g0_done, 1)

            def norms(t):
                n = rows(t)
                pool.wait_ge(mv_ready, t + 1)
                steps = ((small[0:n, 0:1], mv[0:n, 1:2], eps_col[0:n], ALU.add),
                         (rstd[0:n, 0:1], small[0:n, 0:1], minus_half[0:n], ALU.pow),
                         (small[0:n, 1:2], rstd[0:n, 0:1], rstd[0:n, 0:1], ALU.mult),
                         (small[0:n, 2:3], small[0:n, 1:2], mv[0:n, 1:2], ALU.mult),
                         (small[0:n, 3:4], small[0:n, 2:3], eps_col[0:n], ALU.add))
                for i, (dst, a, b, op) in enumerate(steps):
                    pool.tensor_tensor(dst, a, b, op).then_inc(rstd_step, 1)
                    pool.wait_ge(rstd_step, len(steps) * t + i + 1)
                pool.tensor_tensor(rstd[0:n, 1:2], small[0:n, 3:4], minus_half[0:n], ALU.pow).then_inc(rstd_ready, 1)

            def final_norm(t):
                n = rows(t)
                pool.wait_ge(fmv_ready, t + 1)
                pool.tensor_tensor(fvar[0:n], fmv[0:n, 1:2], eps_col[0:n], ALU.add).then_inc(frstd_step, 1)
                pool.wait_ge(frstd_step, t + 1)
                pool.tensor_tensor(frstd[0:n], fvar[0:n], minus_half[0:n], ALU.pow).then_inc(frstd_ready, 1)

            def slot(t):
                if there(t):
                    last_agreement(t)
                if there(t - 2):
                    norms(t - 2)
                if there(t - 4):
                    final_norm(t - 4)

            slot(0)
            bias_split()
            for t in range(1, LOOP.start):
                slot(t)
            with pool.Fori(LOOP.start, LOOP.stop) as t:
                slot(t)
            for t in range(LOOP.stop, TILES + 4):
                slot(t)

        @block.tensor
        def _(pe):
            mm = pe.matmul
            pe.wait_ge(consts, 2)
            pe.wait_ge(w_in, 16)
            for j, bank in enumerate((bank_y, bank_z, bank_v)):
                for k in (2 * j, 2 * j + 1):
                    for e in range(E2):
                        at = (k % 2) * D + e * 128
                        last = pe.transpose(bank[:, at:at + 128], w_rows[:, e, k * 128:(k + 1) * 128], ident[:])
                last.then_inc(wT_psum, 1)

            def turn_block(n):
                pe.wait_ge(x_pat_ready, n + 1)
                for ih, banks in enumerate((bank_bc, bank_cd)):
                    if n > 0:
                        pe.wait_ge(xT_act if ih else xT_dve, n)
                    for g in range(GRID):
                        last = pe.transpose(banks[:, g // 3, (g % 3) * HR:(g % 3 + 1) * HR],
                                            x_pat[:, n % 2, g, ih * 128:(ih + 1) * 128], ident[0:HR, 0:HR])
                    last.then_inc(xT_psum, 1)

            def project(c):
                for e, bank in enumerate((bank_y, bank_z)):
                    if c > 0:
                        pe.wait_ge(hT_ready, E2 * (c - 1) + e + 1)
                    for k in range(KT):
                        last = mm(bank[:, 0:CP], wT[:, k, e * 128:(e + 1) * 128], xT[:, k, c * CP:(c + 1) * CP],
                                  start=(k == 0), stop=(k == KT - 1))
                    last.then_inc(tok_psum, 1)

            def project_paths(c):
                pe.wait_ge(hT_ready, E2 * (c + 1))
                if c > 0:
                    pe.wait_ge(path_f_ready, c)
                for e in range(E2):
                    last = mm(bank_o[0:HD, 0:CT], wvp[:, e, D:D + HD], hT[:, e, c * CT:(c + 1) * CT],
                              start=(e == 0), stop=(e == E2 - 1))
                last.then_inc(path_psum, 1)

            def values_and_paths(t):
                n = rows(t)
                pe.wait_ge(hT_proj_in, 16 * (t + 1))
                if counts(t):
                    pe.wait_ge(v_ready, t)
                    pe.wait_ge(path_k_ready, t)
                mm(bank_v[0:n, 0:D + HD], hT_proj[:, 0, 0:n], wvp[:, 0, :], start=True, stop=False)
                mm(bank_v[0:n, 0:D + HD], hT_proj[:, 1, 0:n], wvp[:, 1, :], start=False, stop=False)
                mm(bank_v[0:n, D:D + HD], ones_row[:, 0:n], bp_row_dh[:], start=False, stop=True).then_inc(proj_done, 1)

            def broadcast_paths(t, second, first_half=False):
                n = rows(t)
                k = PARTS * HALF if first_half else HALF_AT + PARTS * HALF
                if second:
                    pe.wait_ge(uA_done, t + 1)
                elif counts(t):
                    pe.wait_ge(uB_done, t)
                for j in range(2):
                    at = (2 * second + j) * BR * T
                    last = mm(bank_bc[0:n, j, 0:BR * T], pick[0:k, bass.ds(t * R, n)], q_parts[0:k, at:at + BR * T],
                              start=True, stop=True)
                last.then_inc(bcB_done if second else bcA_done, 1)

            def weigh(t):
                n = rows(t)
                pe.wait_ge(probs_ready, t + 1)
                pe.wait_ge(v_ready, t + 1)
                if counts(t):
                    pe.wait_ge(ctx_ready, t)
                for h in range(H):
                    last = mm(bank_ctx[0:n, h * (DH + 1):(h + 1) * (DH + 1)],
                              probs[0:n, h, 0:images(t), :].rearrange("p b q -> p (b q)"), v_ones[0:n, h, :],
                              start=True, stop=True)
                last.then_inc(pv_done, 1)

            def turn_ctx(t):
                n = rows(t)
                pe.wait_ge(ctx_ready, t + 1)
                if counts(t - 1):
                    pe.wait_ge(hnT_ready, t - 1)
                for e in range(E2):
                    last = pe.transpose(bank_turn[:, e * R:e * R + n], ctx_rows[0:n, e * 128:(e + 1) * 128],
                                        ident[0:n, 0:n])
                last.then_inc(ctxT_psum, 1)

            def output_product(t):
                n = rows(t)
                pe.wait_ge(ctxT_ready, t + 1)
                pe.wait_ge(hT_res_in, 16 * (t + 1))
                if counts(t):
                    pe.wait_ge(h2_ready, t)
                else:
                    pe.wait_ge(path_f_ready, CHUNKS)
                mm(bank_o[0:n, 0:D], ctxT[:, 0, 0:n], wo[:, 0, :], start=True, stop=False)
                mm(bank_o[0:n, 0:D], ctxT[:, 1, 0:n], wo[:, 1, :], start=False, stop=False)
                mm(bank_o[0:n, 0:128], hT_res[:, 0, 0:n], ident[:], start=False, stop=False)
                mm(bank_o[0:n, 128:D], hT_res[:, 1, 0:n], ident[:], start=False, stop=True).then_inc(wo_done, 1)

            def turn_normed(t):
                n = rows(t)
                pe.wait_ge(n2_ready, t + 1)
                if there(t + 1):
                    pe.wait_ge(ctxT_ready, t + 2)
                else:
                    pe.wait_ge(hnT_ready, t)
                for e in range(E2):
                    last = pe.transpose(bank_turn[:, e * R:e * R + n], n2[0:n, e * 128:(e + 1) * 128], ident[0:n, 0:n])
                last.then_inc(n2T_psum, 1)

            def hidden(t, q):
                n = rows(t)
                if q == 0:
                    pe.wait_ge(hnT_ready, t + 1)
                if counts(2 * t + q):
                    pe.wait_ge(act_ready, 2 * t + q)
                for i in range(FQ):
                    f = q * FQ + i
                    for e in range(E2):
                        mm(bank_y[:, i * R:i * R + n], w1[:, e, f * 128:(f + 1) * 128],
                           hnT[:, e, bass.ds(t * R, n)], start=(e == 0), stop=False)
                    last = mm(bank_y[:, i * R:i * R + n], bias_parts[:, f * 128:(f + 1) * 128], ones_bf[:, 0:n],
                              start=False, stop=True)
                last.then_inc(y_psum, 1)

            def feed_forward_output(t):
                n = rows(t)
                if counts(t):
                    pe.wait_ge(res_ready, t)
                for f in range(FB):
                    if f % FQ == 0:
                        pe.wait_ge(act_ready, 2 * t + f // FQ + 1)
                    mm(bank_z[0:n, 0:D], act2[:, f, 0:n], w2[:, f, :], start=(f == 0), stop=False)
                mm(bank_z[0:n, 0:D], half_bf[:, 0:n], bias_parts[:, F:F + D], start=False, stop=True).then_inc(z_psum, 1)

            def slot(t, first_half=False):
                if there(t):
                    broadcast_paths(t, 1, first_half)
                if there(t - 3):
                    hidden(t - 3, 0)
                if there(t - 1):
                    weigh(t - 1)
                if there(t - 3):
                    hidden(t - 3, 1)
                if there(t - 1):
                    turn_ctx(t - 1)
                if there(t + 1):
                    values_and_paths(t + 1)
                if there(t - 3):
                    feed_forward_output(t - 3)
                if there(t + 1):
                    broadcast_paths(t + 1, 0, first_half)
                if there(t - 1):
                    output_product(t - 1)
                if there(t - 2):
                    turn_normed(t - 2)

            turn_block(0)
            turn_block(1)
            pe.wait_ge(par_in, 16 * N_PAR)
            for e in range(E2):
                pe.transpose(bank_o[:, e * T:(e + 1) * T], pos_rows[:, e * 128:(e + 1) * 128], ident[0:T, 0:T])
            pe.transpose(bank_o[:, E2 * T:E2 * T + N_VEC], vec_rows[:], ident[0:N_VEC, 0:N_VEC]).then_inc(pos_psum, 1)
            pe.wait_ge(colwise, 1)
            pe.transpose(bank_o[0:HD, E2 * T + N_VEC:E2 * T + N_VEC + 1], bp_row_dh[:], ident[0:1, 0:1]).then_inc(pos_psum, 1)
            turn_block(2)
            pe.wait_ge(wT_ready, 3)
            pe.wait_ge(xT_dve, C)
            pe.wait_ge(xT_act, C)
            project(0)
            project(1)
            pe.wait_ge(cls_ready, E2)
            pe.wait_ge(colwise, 3)
            project_paths(0)
            turn_block(3)
            project_paths(1)
            turn_block(4)
            turn_block(5)
            pe.wait_ge(mats_in, 16 * N_MATS)
            pe.wait_ge(consts, N_CONST)
            pe.wait_ge(xT_dve, 2 * C)
            pe.wait_ge(q_parts_in, 16)
            slot(-1, first_half=True)
            pe.wait_ge(xT_act, 2 * C)
            project(2)
            slot(0, first_half=True)
            project_paths(2)
            project(3)
            project_paths(3)
            slot(1, first_half=True)
            slot(2, first_half=True)
            pe.wait_ge(dequant, 2)
            pe.wait_ge(bias_step, 8)
            slot(3, first_half=True)
            pe.wait_ge(q_parts_in, 32)
            with pe.Fori(LOOP.start, LOOP.stop) as t:
                slot(t)
            for t in range(LOOP.stop, TILES + 3):
                slot(t)

        @block.scalar
        def _(act):
            for dst, src in (
                (pos_rows[:], pos.rearrange("o t d -> (o t) d")),
                (vec_rows[0:E2], tok_b.rearrange("(e p) -> e p", p=128)),
                (vec_rows[E2:2 * E2], cls_token.rearrange("o q (e p) -> (o q e) p", p=128)),
                (vec_rows[2 * E2:3 * E2], ln_gamma.rearrange("(e p) -> e p", p=128)),
                (vec_rows[3 * E2:4 * E2], ln_beta.rearrange("(e p) -> e p", p=128)),
                (bp_row[:], bp.rearrange("(o n) -> o n", o=1)),
                (wp_dh[:], Wp.rearrange("(e p) n -> p e n", p=128)),
            ):
                act.dma_start(dst, src).then_inc(par_in, 16)
            act.preload_act_table(ACT.Exp)

            def x_columns(n):
                act.wait_ge(xT_psum, 2 * n + 2)
                half, c = divmod(n, C)
                dst = xT[:, 2 * c + 1, half * HR * GRID:(half + 1) * HR * GRID].rearrange("p (r a g) -> p a g r", a=2, g=3)
                src = bank_cd[:, :, 0:3 * HR].rearrange("p a (g r) -> p a g r", g=3)
                act.activation(dst, src, ACT.Copy).then_inc(xT_act, 1)

            def paths(c):
                act.wait_ge(path_psum, c + 1)
                if c > 0:
                    act.wait_ge(split_step, 3 * c - 2)
                act.activation(path_f[:], bank_o[0:HD, 0:CT], ACT.Tanh, scale=0.5, bias=bp_half[:]).then_inc(path_f_ready, 1)
                act.wait_ge(path_f_ready, c + 1)
                if c >= 2:
                    act.wait_ge(path_out, 16 * PARTS * (c - 1))
                act.activation(path_parts[:, c % 2, 0, :], path_f[:], ACT.Copy, scale=0.5).then_inc(path_hi_ready, 1)

            def own_paths(t):
                n = rows(t)
                act.wait_ge(proj_done, t + 1)
                if counts(t):
                    act.wait_ge(uB_done, t)
                act.activation(path_k[0:n, :], bank_v[0:n, D:D + HD], ACT.Tanh, scale=0.5).then_inc(path_k_ready, 1)

            def agreements(t):
                n = rows(t)
                act.wait_ge(uA_done, t + 1)
                act.activation(agree[0:n, H:2 * BR, :], agree[0:n, H:2 * BR, :], ACT.Copy, bias=0.5).then_inc(gA_done, 1)
                act.wait_ge(uB_done, t + 1)
                act.activation(agree[0:n, 2 * BR:4 * H, :], agree[0:n, 2 * BR:4 * H, :], ACT.Copy,
                               bias=0.5).then_inc(gB_done, 1)

            def values(t):
                n = rows(t)
                act.wait_ge(proj_done, t + 1)
                if counts(t):
                    act.wait_ge(pv_done, t)
                act.activation(v_ones[0:n, :, 0:DH], bank_v[0:n, 0:D].rearrange("p (h d) -> p h d", h=H),
                               ACT.Copy).then_inc(v_ready, 1)

            def exponentials(t):
                n = rows(t)
                act.wait_ge(sim_ready, t + 1)
                if counts(t):
                    act.wait_ge(pv_done, t)
                for b in range(images(t)):
                    last = act.activation(probs[0:n, :, b, :], sim[0:n], ACT.Exp, scale=1.0 / DEPTH,
                                          bias=own_image[0:n, b:b + 1])
                last.then_inc(probs_ready, 1)

            def ctx_columns(t):
                n = rows(t)
                act.wait_ge(ctxT_psum, t + 1)
                if counts(t):
                    act.wait_ge(wo_done, t)
                act.activation(ctxT[:, :, 0:n], bank_turn[:, 0:E2 * R].rearrange("p (e r) -> p e r", e=E2)[:, :, 0:n],
                               ACT.Copy).then_inc(ctxT_ready, 1)

            def normed_columns(t):
                n = rows(t)
                act.wait_ge(n2T_psum, t + 1)
                for e in range(E2):
                    last = act.activation(hnT[:, e, bass.ds(t * R, n)], bank_turn[:, e * R:e * R + n], ACT.Identity,
                                          scale=gamma_col[:, e:e + 1], bias=beta_col[:, e:e + 1])
                last.then_inc(hnT_ready, 1)

            def half_tanh(t, q):
                n = rows(t)
                act.wait_ge(y_psum, 2 * t + q + 1)
                act.activation(th[:, q, :, 0:n], bank_y[:, 0:FQ * R].rearrange("p (f n) -> p f n", f=FQ)[:, :, 0:n],
                               ACT.Tanh, scale=0.5).then_inc(th_ready, 1)

            def slot(t):
                if there(t):
                    agreements(t)
                if there(t - 3):
                    half_tanh(t - 3, 0)
                if there(t):
                    values(t)
                    exponentials(t)
                if there(t - 3):
                    half_tanh(t - 3, 1)
                if there(t - 1):
                    ctx_columns(t - 1)
                if there(t + 1):
                    own_paths(t + 1)
                if there(t - 2):
                    normed_columns(t - 2)

            x_columns(0)
            x_columns(1)
            x_columns(2)
            act.wait_ge(colwise, 3)
            paths(0)
            x_columns(3)
            paths(1)
            x_columns(4)
            x_columns(5)
            act.wait_ge(consts, N_CONST)
            slot(-1)
            slot(0)
            paths(2)
            paths(3)
            slot(1)
            act.wait_ge(q_in, 16 * N_Q)
            act.activation(s2[:], s2[:], ACT.Copy, scale=0.25).then_inc(s2_ready, 1)
            slot(2)
            slot(3)
            with act.Fori(LOOP.start, LOOP.stop) as t:
                slot(t)
            for t in range(LOOP.stop, TILES + 3):
                slot(t)

        @block.vector
        def _(dve):
            tt, ts, stt = dve.tensor_tensor, dve.tensor_scalar, dve.scalar_tensor_tensor
            for j, bank in enumerate((bank_y, bank_z, bank_v)):
                dve.wait_ge(wT_psum, j + 1)
                dve.tensor_copy(wT[:, 2 * j:2 * j + 2, :], bank[:].rearrange("p (k d) -> p k d", k=2)).then_inc(wT_ready, 1)

            def by_patch(n):
                dve.wait_ge(x_in[n], 16)
                if n >= 2:
                    dve.wait_ge(xT_psum, 2 * n - 2)
                dve.tensor_copy(x_pat[:, n % 2].rearrange("p g (i j) -> p g i j", i=PATCH),
                                x_rows[:, n, :].rearrange("p (i g j) -> p g i j", i=PATCH, g=GRID)).then_inc(x_pat_ready, 1)

            def x_columns(n):
                dve.wait_ge(xT_psum, 2 * n + 1)
                half, c = divmod(n, C)
                dst = xT[:, 2 * c, half * HR * GRID:(half + 1) * HR * GRID].rearrange("p (r a g) -> p a g r", a=2, g=3)
                src = bank_bc[:, :, 0:3 * HR].rearrange("p a (g r) -> p a g r", g=3)
                dve.tensor_copy(dst, src).then_inc(xT_dve, 1)

            def tokens(c):
                for e, bank in enumerate((bank_y, bank_z)):
                    dve.wait_ge(tok_psum, E2 * c + e + 1)
                    tt(image_rows(hT[:, e, c * CT:(c + 1) * CT], T)[:, :, 1:T], image_rows(bank[:, 0:CP], NP),
                       spread(posb[:, e, 1:T], CI), ALU.add).then_inc(hT_ready, 1)

            def split_paths(c):
                dve.wait_ge(path_hi_ready, c + 1)
                if c > 0:
                    dve.wait_ge(split_step, 3 * c)
                stt(out=path_rest[:], in0=path_f[:], scalar=0.5, in1=path_parts[:, c % 2, 0, :], op0=ALU.mult,
                    op1=ALU.subtract).then_inc(split_step, 1)
                dve.wait_ge(split_step, 3 * c + 1)
                dve.tensor_copy(path_parts[:, c % 2, 1, :], path_rest[:]).then_inc(split_step, 1)
                dve.wait_ge(split_step, 3 * c + 2)
                tt(path_parts[:, c % 2, 2, :], path_rest[:], path_parts[:, c % 2, 1, :], ALU.subtract).then_inc(split_step, 1)

            def products(t, second):
                n = rows(t)
                if second:
                    dve.wait_ge(bcB_done, t + 1)
                else:
                    dve.wait_ge(bcA_done, t + 1)
                    dve.wait_ge(path_k_ready, t + 1)
                r = slice(second * 2 * BR, (second + 1) * 2 * BR)
                tt(agree[0:n, r, :].rearrange("p (k r) q -> p k r q", k=2),
                   bank_bc[0:n, :, 0:BR * T].rearrange("p k (r q) -> p k r q", q=T),
                   path_k[0:n, r].rearrange("p (k r o) -> p k r o", k=2, o=1).broadcast_to([n, 2, BR, T]),
                   ALU.mult).then_inc(uB_done if second else uA_done, 1)

            def similarities(t):
                n = rows(t)

                def depth(j):
                    return agree[0:n, j * H:(j + 1) * H, :].rearrange("p h q -> p (h q)")

                def part(i):
                    return horner[0:n, i, :]

                dve.wait_ge(gA_done, t + 1)
                stt(out=part(0), in0=depth(0), scalar=1.5, in1=depth(1), op0=ALU.add, op1=ALU.mult).then_inc(horner_step, 1)
                dve.wait_ge(gB_done, t + 1)
                dve.wait_ge(horner_step, 3 * t + 1)
                stt(out=part(1), in0=part(0), scalar=1.0, in1=depth(2), op0=ALU.add, op1=ALU.mult).then_inc(horner_step, 1)
                dve.wait_ge(horner_step, 3 * t + 2)
                stt(out=part(0), in0=part(1), scalar=1.0, in1=depth(3), op0=ALU.add, op1=ALU.mult).then_inc(horner_step, 1)
                dve.wait_ge(g0_done, t + 1)
                dve.wait_ge(horner_step, 3 * t + 3)
                if counts(t):
                    dve.wait_ge(probs_ready, t)
                stt(out=sim[0:n].rearrange("p h q -> p (h q)"), in0=part(0), scalar=1.0, in1=depth(4), op0=ALU.add,
                    op1=ALU.mult).then_inc(sim_ready, 1)

            def normalise_ctx(t):
                n = rows(t)
                weighted = bank_ctx[0:n, 0:H * (DH + 1)].rearrange("p (h d) -> p h d", h=H)
                dve.wait_ge(pv_done, t + 1)
                dve.reciprocal(recip[0:n, :], weighted[:, :, DH]).then_inc(recip_done, 1)
                dve.wait_ge(recip_done, t + 1)
                if counts(t):
                    dve.wait_ge(ctxT_psum, t)
                tt(ctx_rows[0:n, :].rearrange("p (h d) -> p h d", h=H), weighted[:, :, 0:DH],
                   recip[0:n, :].rearrange("p (h o) -> p h o", o=1).broadcast_to([n, H, DH]), ALU.mult).then_inc(ctx_ready, 1)

            def measure(t):
                n = rows(t)
                dve.wait_ge(wo_done, t + 1)
                dve.bn_stats(stats[0:n, :], bank_o[0:n, 0:D])
                dve.drain()
                dve.bn_aggr(mv[0:n, :], stats[0:n, :]).then_inc(mv_ready, 1)

            def normalise(t):
                n = rows(t)
                dve.wait_ge(rstd_ready, t + 1)
                row = h2[0:n, bass.ds(t, 1), :].rearrange("p o d -> p (o d)")
                ts(row, bank_o[0:n, 0:D], mv[0:n, 0:1], rstd[0:n, 0:1], ALU.subtract, ALU.mult).then_inc(h2_ready, 1)
                dve.wait_ge(h2_ready, t + 1)
                if counts(t):
                    dve.wait_ge(n2T_psum, t)
                ts(n2[0:n, :], row, rstd[0:n, 1:2], None, ALU.mult).then_inc(n2_ready, 1)

            def silu(t, q):
                n = rows(t)
                dve.wait_ge(th_ready, 2 * t + q + 1)
                if counts(t):
                    dve.wait_ge(z_psum, t)
                stt(out=act2[:, q * FQ:(q + 1) * FQ, 0:n], in0=th[:, q, :, 0:n], scalar=1.0,
                    in1=bank_y[:, 0:FQ * R].rearrange("p (f n) -> p f n", f=FQ)[:, :, 0:n], op0=ALU.add,
                    op1=ALU.mult).then_inc(act_ready, 1)

            def residual(t):
                n = rows(t)
                dve.wait_ge(z_psum, t + 1)
                if counts(t):
                    dve.wait_ge(fin_ready, t)
                row = h2[0:n, bass.ds(t, 1), :].rearrange("p o d -> p (o d)")
                stt(out=res[0:n, :], in0=row, scalar=2.0, in1=bank_z[0:n, 0:D], op0=ALU.mult,
                    op1=ALU.add).then_inc(res_ready, 1)
                dve.wait_ge(res_ready, t + 1)
                dve.bn_stats(fstats[0:n, :], res[0:n, :])
                dve.drain()
                dve.bn_aggr(fmv[0:n, :], fstats[0:n, :]).then_inc(fmv_ready, 1)

            def final(t):
                n = rows(t)
                dve.wait_ge(frstd_ready, t + 1)
                if counts(t):
                    dve.wait_ge(stored, 16 * t)
                ts(fin[0:n, :], res[0:n, :], fmv[0:n, 0:1], frstd[0:n, 0:1], ALU.subtract, ALU.mult).then_inc(fin_ready, 1)

            def slot(t):
                if there(t):
                    products(t, 1)
                if there(t - 2):
                    measure(t - 2)
                if there(t - 4):
                    residual(t - 4)
                if there(t):
                    similarities(t)
                if there(t - 3):
                    silu(t - 3, 0)
                if there(t - 1):
                    normalise_ctx(t - 1)
                if there(t - 2):
                    normalise(t - 2)
                if there(t - 3):
                    silu(t - 3, 1)
                if there(t - 4):
                    final(t - 4)
                if there(t + 1):
                    products(t + 1, 0)

            by_patch(0)
            by_patch(1)
            x_columns(0)
            by_patch(2)
            x_columns(1)
            dve.wait_ge(par_in, 16 * N_PAR)
            for j in range(DEPTH):
                d = DEPTH - 1 - j
                dve.tensor_copy(bp_row_dh[:, j * H:(j + 1) * H], bp_row[:].rearrange("o (h d) -> o h d", d=DEPTH)[:, :, d])
                last = dve.tensor_copy(wvp[:, :, D + j * H:D + (j + 1) * H],
                                       wp_dh[:].rearrange("p e (h d) -> p e h d", d=DEPTH)[:, :, :, d])
            last.then_inc(colwise, 1)
            dve.wait_ge(pos_psum, 2)
            dve.tensor_copy(vec_cols[:], bank_o[:, E2 * T:E2 * T + N_VEC]).then_inc(colwise, 1)
            ts(bp_half[:], bank_o[0:HD, E2 * T + N_VEC:E2 * T + N_VEC + 1], 0.5, None, ALU.mult).then_inc(colwise, 1)
            dve.wait_ge(colwise, 2)
            for e in range(E2):
                ts(posb[:, e, 1:T], bank_o[:, e * T + 1:(e + 1) * T], tokb_col[:, e:e + 1], None, ALU.add)
                tt(posb[:, e, 0:1], bank_o[:, e * T:e * T + 1], cls_col[:, e:e + 1], ALU.add).then_inc(posb_step, 1)
            x_columns(2)
            dve.wait_ge(posb_step, E2)
            for e in range(E2):
                dve.tensor_copy(image_rows(hT[:, e, :], T)[:, :, 0], posb[:, e, 0:1].broadcast_to([128, B])).then_inc(cls_ready, 1)
            by_patch(3)
            tokens(0)
            by_patch(4)
            tokens(1)
            split_paths(0)
            x_columns(3)
            by_patch(5)
            split_paths(1)
            x_columns(4)
            x_columns(5)
            slot(-1)
            tokens(2)
            slot(0)
            split_paths(2)
            tokens(3)
            split_paths(3)
            slot(1)
            dve.wait_ge(q_in, 16 * N_Q)
            stt(out=w1[:], in0=q1[:], scalar=-ZERO_POINT, in1=s1[:], op0=ALU.add, op1=ALU.mult).then_inc(dequant, 1)
            slot(2)
            dve.wait_ge(s2_ready, 1)
            stt(out=w2[:], in0=q2[:], scalar=-ZERO_POINT, in1=s2[:], op0=ALU.add, op1=ALU.mult).then_inc(dequant, 1)
            slot(3)
            with dve.Fori(LOOP.start, LOOP.stop) as t:
                slot(t)
            for t in range(LOOP.stop, TILES + 4):
                slot(t)


_INS = ["x", "L0_tok_W", "L0_tok_b", "L0_tok_cls_token", "L0_tok_pos_embedding", "L0_attn_Wp", "L0_attn_bp",
        "L0_attn_Wv", "L0_attn_Wo", "L0_ffn_ln_gamma", "L0_ffn_ln_beta", "L0_ffn_fc1_q", "L0_ffn_fc1_scales",
        "L0_ffn_fc1_bias", "L0_ffn_fc2_q", "L0_ffn_fc2_scales", "L0_ffn_fc2_bias"]


def kernel(**inputs):
    import numpy as np
    import concourse.bacc as bacc
    from concourse.bass_utils import run_bass_kernel_spmd

    nc = bacc.Bacc("TRN2", target_bir_lowering=False, num_devices=1)
    arrays, args = {}, []
    for name in _INS:
        a = np.ascontiguousarray(inputs[name])
        arrays[f"in_{name}"] = a
        args.append(nc.dram_tensor(f"in_{name}", a.shape, mybir.dt.from_np(a.dtype), kind="ExternalInput").ap())
    B = inputs["x"].shape[0]
    _, T, D = inputs["L0_tok_pos_embedding"].shape
    args.append(nc.dram_tensor("out_0", (B, T, D), F32, kind="ExternalOutput").ap())
    vit_block(nc, *args)
    r = run_bass_kernel_spmd(nc, [arrays], core_ids=[0])
    return r.results[0]["out_0"]
```

```python
from contextlib import ExitStack

import concourse.bass as bass
from concourse import mybir

ALU = mybir.AluOpType
ACT = mybir.ActivationFunctionType
F32 = mybir.dt.float32
BF16 = mybir.dt.bfloat16
I32 = mybir.dt.int32
EPS = 1e-5
MASKED = -1e4
ZERO_POINT = 128.0


def vit_block(nc, x, tok_W, tok_b, cls_token, pos, Wp, bp, Wv, Wo, ln_gamma, ln_beta,
              fc1_q, fc1_scales, fc1_bias, fc2_q, fc2_scales, fc2_bias, out):
    B, C, IMG, _ = x.shape
    D, PATCH_DIM = tok_W.shape
    T = pos.shape[1]
    NP = T - 1
    PATCH = 16
    GRID = IMG // PATCH
    KT = PATCH_DIM // 128
    E2 = D // 128
    HALF = B // 2
    HR = HALF * GRID
    HD = Wp.shape[1]
    H = 8
    DEPTH = HD // H
    DH = D // H
    NTOK = B * T
    IT = 3
    R = IT * T
    TILES = -(-B // IT)
    CI = 8
    CHUNKS = B // CI
    CP, CT = CI * NP, CI * T
    F = fc1_q.shape[1]
    FB = F // 128
    FQ = FB // 2
    G1, G2 = fc1_scales.shape[0], fc2_scales.shape[0]
    BR = HD // 4
    UROWS = HD * T
    PARTS = 3
    WARM_UP = 8
    HALF_AT = 64

    def images(t):
        return min(IT, B - t * IT) if isinstance(t, int) else IT

    def rows(t):
        return images(t) * T

    def there(t):
        return not isinstance(t, int) or 0 <= t < TILES

    def counts(n):
        return not isinstance(n, int) or n > 0

    with ExitStack() as ctx:
        def sb(name, shape, dt=F32):
            return ctx.enter_context(nc.sbuf_tensor(name, shape, dt))

        def ps(name, shape):
            return ctx.enter_context(nc.psum_tensor(name, shape, F32))

        def sem(name):
            return ctx.enter_context(nc.semaphore(name))

        bank_bc = ps("bank_bc", [128, 2, 512])
        bank_cd = ps("bank_cd", [128, 2, 512])
        bank_ctx, bank_turn = bank_cd[:, 0, :], bank_cd[:, 1, :]
        bank_y = ps("bank_y", [128, 512])
        bank_z = ps("bank_z", [128, 512])
        bank_v = ps("bank_v", [128, 512])
        bank_o = ps("bank_o", [128, 512])

        ident = sb("ident", [128, 128])
        x_rows_all = sb("x_rows", [128, 2 * C * PATCH * IMG])
        x_rows = x_rows_all[0:HR, :].rearrange("p (n k) -> p n k", n=2 * C)
        xT = sb("xT", [128, KT, B * NP])
        w_rows = sb("w_rows", [128, E2, PATCH_DIM])
        wT = sb("wT", [128, KT, D])
        pos_rows = sb("pos_rows", [T, D])
        N_VEC = 2 * E2
        tok_rows = sb("tok_rows", [N_VEC, 128])
        tok_cols = sb("tok_cols", [128, N_VEC])
        tokb_col, cls_col = tok_cols[:, 0:E2], tok_cols[:, E2:N_VEC]
        ln_rows = sb("ln_rows", [N_VEC, 128])
        ln_cols = sb("ln_cols", [128, N_VEC])
        gamma_col, beta_col = ln_cols[:, 0:E2], ln_cols[:, E2:N_VEC]
        posb = sb("posb", [128, E2, T])
        hT = sb("hT", [128, E2, NTOK])
        hT_proj = sb("hT_proj", [128, E2, R])
        hT_res = sb("hT_res", [128, E2, R])
        wvp = sb("wvp", [128, E2, D + HD])
        wp_dh = sb("wp_dh", [128, E2, HD])
        bp_half = sb("bp_half", [HD, 1])
        bp_row = sb("bp_row", [1, HD])
        bp_row_dh = sb("bp_row_dh", [1, HD])
        ones_row = sb("ones_row", [1, 128])
        path_f = sb("path_f", [HD, CT])
        path_rest = sb("path_rest", [HD, CT])
        path_parts = sb("path_parts", [HD, 2, PARTS, CT], BF16)
        q_parts = sb("q_parts", [128, UROWS], BF16)
        pick = sb("pick", [128, NTOK], BF16)
        FIRST = CI // IT
        q_first = sb("q_first", [PARTS * CI, UROWS], BF16)
        pick_first = sb("pick_first", [PARTS * CI, FIRST * R], BF16)
        path_k = sb("path_k", [128, HD])
        agree = sb("agree", [128, HD, T])
        causal = sb("causal", [128, T])
        own_image = sb("own_image", [128, IT])
        horner = sb("horner", [128, 2, H * T])
        sim = sb("sim", [128, H, T])
        probs = sb("probs", [128, H, IT, T])
        v_ones = sb("v_ones", [128, H, DH + 1])
        recip = sb("recip", [128, H])
        ctx_rows = sb("ctx_rows", [128, D])
        ctxT = sb("ctxT", [128, E2, R])
        wo = sb("wo", [128, E2, D])
        stats = sb("stats", [128, 6])
        mv = sb("mv", [128, 2])
        small = sb("small", [128, 4])
        rstd = sb("rstd", [128, 2])
        minus_half = sb("minus_half", [128, 1])
        eps_col = sb("eps_col", [128, 1])
        assert TILES * D <= 2 * PATCH * IMG
        patches = sb("patches", [128, 2 * PATCH * IMG])
        x_pat = patches[0:HR, :].rearrange("p (n g k) -> p n g k", n=2, g=GRID)
        h2 = patches[:, 0:TILES * D].rearrange("p (t d) -> p t d", t=TILES)
        n2 = sb("n2", [128, D])
        hnT = sb("hnT", [128, E2, NTOK])
        q1 = sb("q1", [128, G1, F], I32)
        q2 = sb("q2", [128, G2, D], I32)
        s1 = sb("s1", [128, G1, F])
        s2 = sb("s2", [128, G2, D])
        w1 = sb("w1", [128, G1, F])
        w2 = sb("w2", [128, G2, D])
        BIAS = 32 * PARTS
        bias_f, bias_rest = (w.rearrange("p a b -> p (a b)")[0:BIAS, 0:F + D] for w in (w2, hnT))
        bias_mid = sb("bias_mid", [BIAS, F + D], BF16)
        bias_parts = sb("bias_parts", [BIAS, F + D], BF16)
        ones_bf = sb("ones_bf", [BIAS, 128], BF16)
        half_bf = sb("half_bf", [BIAS, 128], BF16)
        th = x_rows_all[:, 0:FB * R].rearrange("p (q f n) -> p q f n", q=2, f=FQ)
        act2 = x_rows_all[:, FB * R:2 * FB * R].rearrange("p (f n) -> p f n", f=FB)
        res = sb("res", [128, D])
        fstats = sb("fstats", [128, 6])
        fmv = sb("fmv", [128, 2])
        fvar = sb("fvar", [128, 1])
        frstd = sb("frstd", [128, 1])
        fin = sb("fin", [128, D])

        path_dram = nc.dram_tensor("path_dram", (CHUNKS, PARTS, CI, HD, T), BF16, kind="Internal").ap()

        w_in = sem("w_in")
        x_in = [sem(f"x_in{i}") for i in range(2 * C)]
        tok_par_in = sem("tok_par_in")
        par_in = sem("par_in")
        mats_in = sem("mats_in")
        q1_in = sem("q1_in")
        q2_in = sem("q2_in")
        s2_in = sem("s2_in")
        bias_in = sem("bias_in")
        consts = sem("consts")
        bias_step = sem("bias_step")
        bias_act = sem("bias_act")
        by_depth = sem("by_depth")
        tok_cols_ready = sem("tok_cols_ready")
        colwise = sem("colwise")
        wT_psum = sem("wT_psum")
        wT_ready = sem("wT_ready")
        pos_psum = sem("pos_psum")
        par_psum = sem("par_psum")
        posb_step = sem("posb_step")
        x_pat_ready = sem("x_pat_ready")
        xT_psum = sem("xT_psum")
        xT_dve = sem("xT_dve")
        xT_act = sem("xT_act")
        tok_psum = sem("tok_psum")
        hT_ready = sem("hT_ready")
        cls_ready = sem("cls_ready")
        path_psum = sem("path_psum")
        path_f_ready = sem("path_f_ready")
        path_hi_ready = sem("path_hi_ready")
        split_step = sem("split_step")
        path_out = [sem(f"path_out{c}") for c in range(CHUNKS)]
        q_first_in = sem("q_first_in")
        q_parts_in = sem("q_parts_in")
        s2_ready = sem("s2_ready")
        dequant = sem("dequant")
        hT_proj_in = sem("hT_proj_in")
        hT_res_in = sem("hT_res_in")
        proj_done = sem("proj_done")
        bcA_done = sem("bcA_done")
        bcB_done = sem("bcB_done")
        path_k_ready = sem("path_k_ready")
        v_ready = sem("v_ready")
        uA_done = sem("uA_done")
        uB_done = sem("uB_done")
        gA_done = sem("gA_done")
        gB_done = sem("gB_done")
        g0_done = sem("g0_done")
        horner_step = sem("horner_step")
        sim_ready = sem("sim_ready")
        probs_ready = sem("probs_ready")
        pv_done = sem("pv_done")
        recip_done = sem("recip_done")
        ctx_ready = sem("ctx_ready")
        ctxT_psum = sem("ctxT_psum")
        ctxT_ready = sem("ctxT_ready")
        wo_done = sem("wo_done")
        mv_ready = sem("mv_ready")
        rstd_step = sem("rstd_step")
        rstd_ready = sem("rstd_ready")
        h2_ready = sem("h2_ready")
        n2_ready = sem("n2_ready")
        n2T_psum = sem("n2T_psum")
        hnT_ready = sem("hnT_ready")
        y_psum = sem("y_psum")
        th_ready = sem("th_ready")
        act_ready = sem("act_ready")
        z_psum = sem("z_psum")
        res_ready = sem("res_ready")
        fmv_ready = sem("fmv_ready")
        frstd_step = sem("frstd_step")
        frstd_ready = sem("frstd_ready")
        fin_ready = sem("fin_ready")
        stored = sem("stored")

        N_CONST = 31
        N_TOK_PAR, N_PAR, N_MATS = 3, 4, 2
        LOOP = range(4, TILES - 2)
        out_flat = out.rearrange("b t d -> (b t) d")


        def image_rows(ap, n):
            return ap.rearrange("p (b t) -> p b t", t=n)

        def spread(ap, n):
            return ap.rearrange("p (o t) -> p o t", o=1).broadcast_to([ap.shape[0], n, ap.shape[1]])

        block = ctx.enter_context(nc.Block())

        @block.sync
        def _(sp):
            sp.dma_start(w_rows[:], tok_W.rearrange("(e p) k -> p e k", p=128)).then_inc(w_in, 16)
            for half in range(2):
                for c in range(C):
                    n = half * C + c
                    src = x[half * HALF:(half + 1) * HALF, c].rearrange("b (g i) w -> b g (i w)", i=PATCH)
                    sp.dma_start(x_rows[:, n, :], src).then_inc(x_in[n], 16)
            sp.dma_start(wvp[:, :, 0:D], Wv.rearrange("(e p) n -> p e n", p=128)).then_inc(mats_in, 16)
            sp.dma_start(wo[:], Wo.rearrange("(e p) n -> p e n", p=128)).then_inc(mats_in, 16)
            sp.dma_start(q1[:], fc1_q.rearrange("(g p) n -> p g n", p=128)).then_inc(q1_in, 16)
            sp.dma_start(s1[:], fc1_scales.rearrange("(o g) n -> o g n", o=1).broadcast_to([128, G1, F])).then_inc(q1_in, 16)
            sp.wait_ge(bias_step, 1)
            for part in range(PARTS):
                p = 32 * part
                sp.dma_start(bias_f[p:p + 1, 0:F], fc1_bias.rearrange("(o n) -> o n", o=1)).then_inc(bias_in, 16)
                sp.dma_start(bias_f[p:p + 1, F:F + D], fc2_bias.rearrange("(o n) -> o n", o=1)).then_inc(bias_in, 16)


            def path_part_out(c, part):
                if part == 0:
                    sp.wait_ge(path_hi_ready, c + 1)
                else:
                    sp.wait_ge(split_step, 3 * c + part + 1)
                sp.dma_start(path_dram[c, part].rearrange("b r t -> r b t"),
                             image_rows(path_parts[:, c % 2, part, :], T)).then_inc(path_out[c], 16)

            def paths_in(half):
                pair = CHUNKS // 2
                for c in range(half * pair, (half + 1) * pair):
                    sp.wait_ge(path_out[c], 16 * PARTS)
                sp.dma_start(q_parts[half * HALF_AT:half * HALF_AT + PARTS * HALF, :],
                             path_dram[half * pair:(half + 1) * pair].rearrange("c n b r t -> (c n b) (r t)")
                             ).then_inc(q_parts_in, 16)

            def load_proj(t):
                if counts(t):
                    sp.wait_ge(proj_done, t)
                sp.dma_start(hT_proj[:, :, 0:rows(t)],
                             hT[:, :, bass.ds(t * R, rows(t))]).then_inc(hT_proj_in, 16)

            def load_res(t):
                if counts(t):
                    sp.wait_ge(wo_done, t)
                sp.dma_start(hT_res[:, :, 0:rows(t)],
                             hT[:, :, bass.ds(t * R, rows(t))]).then_inc(hT_res_in, 16)

            def store(t):
                n = rows(t)
                sp.wait_ge(fin_ready, t + 1)
                sp.dma_start(out_flat[bass.ds(t * R, n), :], fin[0:n, :]).then_inc(stored, 16)

            def slot(t):
                if there(t + 2):
                    load_proj(t + 2)
                if there(t):
                    load_res(t)
                if there(t - 4):
                    store(t - 4)

            sp.wait_ge(hT_ready, E2)
            sp.wait_ge(cls_ready, E2)
            load_proj(0)
            load_res(0)
            for part in range(PARTS):
                path_part_out(0, part)
            sp.wait_ge(path_out[0], 16 * PARTS)
            sp.dma_start(q_first[:], path_dram[0].rearrange("n b r t -> (n b) (r t)")).then_inc(q_first_in, 16)
            sp.dma_start(q2[:], fc2_q.rearrange("(g p) n -> p g n", p=128)).then_inc(q2_in, 16)
            load_proj(1)
            for part in range(PARTS):
                path_part_out(1, part)
            sp.wait_ge(consts, N_CONST)
            paths_in(0)
            sp.wait_ge(hT_ready, E2 * CHUNKS // 2)
            load_proj(2)
            sp.dma_start(s2[:], fc2_scales.rearrange("(o g) n -> o g n", o=1).broadcast_to([128, G2, D])).then_inc(s2_in, 16)
            for part in range(PARTS):
                path_part_out(2, part)
            slot(1)
            slot(2)
            for part in range(PARTS):
                path_part_out(3, part)
            paths_in(1)
            sp.wait_ge(hT_ready, E2 * CHUNKS)
            slot(3)
            with sp.Fori(LOOP.start, LOOP.stop - 1) as t:
                slot(t)
            for t in range(LOOP.stop - 1, TILES + 4):
                slot(t)
            sp.wait_ge(stored, 16 * TILES)

        @block.gpsimd
        def _(pool):
            def const(ins):
                ins.then_inc(consts, 1)

            const(pool.memset(ident[:], 1.0))
            pool.wait_ge(consts, 1)
            const(pool.affine_select(out=ident[:], in_=ident[:], compare_op=ALU.is_equal, fill=0.0, base=0,
                                     pattern=[[-1, 128]], channel_multiplier=1))
            const(pool.memset(pick_first[:], 0.0))
            pool.wait_ge(consts, 3)
            for part in range(PARTS):
                some = image_rows(pick_first[:], T)
                const(pool.affine_select(out=some, in_=some, compare_op=ALU.not_equal, fill=1.0,
                                         base=part * CI, pattern=[[1, FIRST * IT], [0, T]], channel_multiplier=-1))
                pool.wait_ge(consts, 4 + part)
            const(pool.memset(q_parts[:], 0.0))
            const(pool.memset(pick[:], 0.0))
            pool.wait_ge(consts, 8)
            for part in range(PARTS):
                for c in range(CHUNKS):
                    half, at = divmod(c, CHUNKS // 2)
                    some = image_rows(pick[half * HALF_AT:(half + 1) * HALF_AT, c * CT:(c + 1) * CT], T)
                    const(pool.affine_select(out=some, in_=some, compare_op=ALU.not_equal, fill=1.0,
                                             base=(at * PARTS + part) * CI, pattern=[[1, CI], [0, T]],
                                             channel_multiplier=-1))
                pool.wait_ge(consts, 8 + CHUNKS * (part + 1))
            const(pool.memset(minus_half[:], -0.5))
            const(pool.memset(eps_col[:], EPS))
            const(pool.memset(ones_row[:], 1.0))
            const(pool.memset(v_ones[:], 1.0))
            const(pool.memset(own_image[:], 0.0))
            pool.wait_ge(consts, 25)
            const(pool.affine_select(out=own_image[:], in_=own_image[:], compare_op=ALU.is_ge, fill=MASKED, base=0,
                                     pattern=[[-T, IT]], channel_multiplier=1))
            pool.wait_ge(consts, 26)
            const(pool.affine_select(out=own_image[:], in_=own_image[:], compare_op=ALU.is_ge, fill=MASKED,
                                     base=T - 1, pattern=[[T, IT]], channel_multiplier=-1))
            const(pool.memset(causal[:], 0.5))
            pool.wait_ge(consts, 28)
            for b in reversed(range(IT)):
                const(pool.affine_select(out=causal[0:T * (b + 1)], in_=causal[0:T * (b + 1)], compare_op=ALU.is_ge,
                                         fill=MASKED, base=T * b, pattern=[[1, T]], channel_multiplier=-1))
                pool.wait_ge(consts, 28 + IT - b)

            def bias_step_done(ins):
                ins.then_inc(bias_step, 1)

            bias_step_done(pool.memset(bias_f, 0.0))
            bias_step_done(pool.memset(ones_bf[:], 1.0))
            bias_step_done(pool.memset(half_bf[:], 0.5))

            pool.wait_ge(bias_act, 1)
            bias_step_done(pool.tensor_tensor(bias_rest, bias_f, bias_parts[:], ALU.subtract))
            pool.wait_ge(bias_act, 3)
            bias_step_done(pool.tensor_tensor(bias_parts[64:96], bias_rest[64:96], bias_mid[64:96], ALU.subtract))
            pool.wait_ge(bias_step, 5)

            def last_agreement(t):
                n = rows(t)
                pool.wait_ge(uB_done, t + 1)
                pool.tensor_tensor(agree[0:n, 4 * H:5 * H, :], agree[0:n, 4 * H:5 * H, :],
                                   spread(causal[0:n, :], H), ALU.add).then_inc(g0_done, 1)

            def norms(t):
                n = rows(t)
                pool.wait_ge(mv_ready, t + 1)
                steps = ((small[0:n, 0:1], mv[0:n, 1:2], eps_col[0:n], ALU.add),
                         (rstd[0:n, 0:1], small[0:n, 0:1], minus_half[0:n], ALU.pow),
                         (small[0:n, 1:2], rstd[0:n, 0:1], rstd[0:n, 0:1], ALU.mult),
                         (small[0:n, 2:3], small[0:n, 1:2], mv[0:n, 1:2], ALU.mult),
                         (small[0:n, 3:4], small[0:n, 2:3], eps_col[0:n], ALU.add))
                for i, (dst, a, b, op) in enumerate(steps):
                    pool.tensor_tensor(dst, a, b, op).then_inc(rstd_step, 1)
                    pool.wait_ge(rstd_step, len(steps) * t + i + 1)
                pool.tensor_tensor(rstd[0:n, 1:2], small[0:n, 3:4], minus_half[0:n], ALU.pow).then_inc(rstd_ready, 1)

            def final_norm(t):
                n = rows(t)
                pool.wait_ge(fmv_ready, t + 1)
                pool.tensor_tensor(fvar[0:n], fmv[0:n, 1:2], eps_col[0:n], ALU.add).then_inc(frstd_step, 1)
                pool.wait_ge(frstd_step, t + 1)
                pool.tensor_tensor(frstd[0:n], fvar[0:n], minus_half[0:n], ALU.pow).then_inc(frstd_ready, 1)

            def slot(t):
                if there(t):
                    last_agreement(t)
                if there(t - 2):
                    norms(t - 2)
                if there(t - 4):
                    final_norm(t - 4)

            for t in range(LOOP.start):
                slot(t)
            with pool.Fori(LOOP.start, LOOP.stop) as t:
                slot(t)
            for t in range(LOOP.stop, TILES + 4):
                slot(t)

        @block.tensor
        def _(pe):
            mm = pe.matmul
            pe.wait_ge(consts, 2)
            for _ in range(WARM_UP):
                pe.transpose(bank_v[:, 0:128], ident[:], ident[:])
            pe.wait_ge(w_in, 16)
            for j, bank in enumerate((bank_y, bank_z, bank_v)):
                for k in (2 * j, 2 * j + 1):
                    for e in range(E2):
                        at = (k % 2) * D + e * 128
                        last = pe.transpose(bank[:, at:at + 128], w_rows[:, e, k * 128:(k + 1) * 128], ident[:])
                last.then_inc(wT_psum, 1)

            def turn_block(n, ih):
                banks = (bank_bc, bank_cd)[ih]
                pe.wait_ge(x_pat_ready, n + 1)
                if n > 0:
                    pe.wait_ge(xT_act if ih else xT_dve, n)
                for g in range(GRID):
                    last = pe.transpose(banks[:, g // 3, (g % 3) * HR:(g % 3 + 1) * HR],
                                        x_pat[:, n % 2, g, ih * 128:(ih + 1) * 128], ident[0:HR, 0:HR])
                last.then_inc(xT_psum, 1)

            def project(c, e, blocks=range(KT)):
                bank = (bank_y, bank_z)[e]
                if c > 0:
                    pe.wait_ge(hT_ready, E2 * (c - 1) + e + 1)
                    if e == 0:
                        pe.wait_ge(path_f_ready, c)
                for k in blocks:
                    last = mm(bank[:, 0:CP], wT[:, k, e * 128:(e + 1) * 128], xT[:, k, c * CP:(c + 1) * CP],
                              start=(k == 0), stop=(k == KT - 1))
                if KT - 1 in blocks:
                    last.then_inc(tok_psum, 1)

            def project_paths(c):
                pe.wait_ge(hT_ready, E2 * (c + 1))
                for e in range(E2):
                    last = mm(bank_y[0:HD, 0:CT], wvp[:, e, D:D + HD], hT[:, e, c * CT:(c + 1) * CT],
                              start=(e == 0), stop=(e == E2 - 1))
                last.then_inc(path_psum, 1)

            def values_and_paths(t):
                n = rows(t)
                pe.wait_ge(hT_proj_in, 16 * (t + 1))
                if counts(t):
                    pe.wait_ge(v_ready, t)
                    pe.wait_ge(path_k_ready, t)
                mm(bank_v[0:n, 0:D + HD], hT_proj[:, 0, 0:n], wvp[:, 0, :], start=True, stop=False)
                mm(bank_v[0:n, 0:D + HD], hT_proj[:, 1, 0:n], wvp[:, 1, :], start=False, stop=False)
                mm(bank_v[0:n, D:D + HD], ones_row[:, 0:n], bp_row_dh[:], start=False, stop=True).then_inc(proj_done, 1)

            def broadcast_paths(t, second):
                n = rows(t)
                if isinstance(t, int) and t < FIRST:
                    chosen, parts = pick_first[:, t * R:(t + 1) * R], q_first[:]
                else:
                    k = PARTS * HALF if isinstance(t, int) and (t + 1) * IT <= HALF else HALF_AT + PARTS * HALF
                    chosen, parts = pick[0:k, bass.ds(t * R, n)], q_parts[0:k, :]
                if second:
                    pe.wait_ge(uA_done, t + 1)
                elif counts(t):
                    pe.wait_ge(uB_done, t)
                for j in range(2):
                    at = (2 * second + j) * BR * T
                    last = mm(bank_bc[0:n, j, 0:BR * T], chosen, parts[:, at:at + BR * T],
                              start=True, stop=True)
                last.then_inc(bcB_done if second else bcA_done, 1)

            def weigh(t):
                n = rows(t)
                pe.wait_ge(probs_ready, t + 1)
                pe.wait_ge(v_ready, t + 1)
                if counts(t):
                    pe.wait_ge(ctx_ready, t)
                for h in range(H):
                    last = mm(bank_ctx[0:n, h * (DH + 1):(h + 1) * (DH + 1)],
                              probs[0:n, h, 0:images(t), :].rearrange("p b q -> p (b q)"), v_ones[0:n, h, :],
                              start=True, stop=True)
                last.then_inc(pv_done, 1)

            def turn_ctx(t):
                n = rows(t)
                pe.wait_ge(ctx_ready, t + 1)
                if counts(t):
                    pe.wait_ge(ctxT_ready, t)
                if counts(t - 1):
                    pe.wait_ge(hnT_ready, t - 1)
                for e in range(E2):
                    last = pe.transpose(bank_turn[:, e * R:e * R + n], ctx_rows[0:n, e * 128:(e + 1) * 128],
                                        ident[0:n, 0:n])
                last.then_inc(ctxT_psum, 1)

            def output_product(t):
                n = rows(t)
                pe.wait_ge(ctxT_ready, t + 1)
                pe.wait_ge(hT_res_in, 16 * (t + 1))
                if counts(t):
                    pe.wait_ge(h2_ready, t)
                mm(bank_o[0:n, 0:D], ctxT[:, 0, 0:n], wo[:, 0, :], start=True, stop=False)
                mm(bank_o[0:n, 0:D], ctxT[:, 1, 0:n], wo[:, 1, :], start=False, stop=False)
                mm(bank_o[0:n, 0:128], hT_res[:, 0, 0:n], ident[:], start=False, stop=False)
                mm(bank_o[0:n, 128:D], hT_res[:, 1, 0:n], ident[:], start=False, stop=True).then_inc(wo_done, 1)

            def turn_normed(t):
                n = rows(t)
                pe.wait_ge(n2_ready, t + 1)
                if counts(t):
                    pe.wait_ge(hnT_ready, t)
                if not there(t + 1):
                    pe.wait_ge(ctxT_ready, t + 1)
                for e in range(E2):
                    last = pe.transpose(bank_turn[:, (E2 + e) * R:(E2 + e) * R + n], n2[0:n, e * 128:(e + 1) * 128],
                                        ident[0:n, 0:n])
                last.then_inc(n2T_psum, 1)

            def hidden(t, q):
                n = rows(t)
                if q == 0:
                    pe.wait_ge(hnT_ready, t + 1)
                if counts(2 * t + q):
                    pe.wait_ge(act_ready, 2 * t + q)
                for i in range(FQ):
                    f = q * FQ + i
                    for e in range(E2):
                        mm(bank_y[:, i * R:i * R + n], w1[:, e, f * 128:(f + 1) * 128],
                           hnT[:, e, bass.ds(t * R, n)], start=(e == 0), stop=False)
                    last = mm(bank_y[:, i * R:i * R + n], bias_parts[:, f * 128:(f + 1) * 128], ones_bf[:, 0:n],
                              start=False, stop=True)
                last.then_inc(y_psum, 1)

            def feed_forward_output(t, q):
                n = rows(t)
                if q == 0 and counts(t):
                    pe.wait_ge(res_ready, t)
                pe.wait_ge(act_ready, 2 * t + q + 1)
                for f in range(q * FQ, (q + 1) * FQ):
                    last = mm(bank_z[0:n, 0:D], act2[:, f, 0:n], w2[:, f, :], start=(f == 0), stop=False)
                if q == 1:
                    last = mm(bank_z[0:n, 0:D], half_bf[:, 0:n], bias_parts[:, F:F + D], start=False, stop=True)
                last.then_inc(z_psum, 1)

            def slot(t, start=None, middle=None):
                if there(t):
                    broadcast_paths(t, 1)
                if start:
                    start()
                if there(t - 3):
                    hidden(t - 3, 0)
                if there(t - 1):
                    weigh(t - 1)
                if there(t - 3):
                    hidden(t - 3, 1)
                if middle:
                    middle()
                if there(t - 1):
                    turn_ctx(t - 1)
                if there(t - 2):
                    turn_normed(t - 2)
                if there(t + 1):
                    values_and_paths(t + 1)
                if there(t - 3):
                    feed_forward_output(t - 3, 0)
                    feed_forward_output(t - 3, 1)
                if there(t + 1):
                    broadcast_paths(t + 1, 0)
                if there(t - 1):
                    output_product(t - 1)

            turn_block(0, 0)
            turn_block(0, 1)
            pe.wait_ge(tok_par_in, 16 * N_TOK_PAR)
            for e in range(E2):
                pe.transpose(bank_o[:, e * T:(e + 1) * T], pos_rows[:, e * 128:(e + 1) * 128], ident[0:T, 0:T])
            pe.transpose(bank_o[:, E2 * T:E2 * T + N_VEC], tok_rows[:], ident[0:N_VEC, 0:N_VEC]).then_inc(pos_psum, 1)
            turn_block(1, 0)
            turn_block(1, 1)
            pe.wait_ge(wT_ready, 3)
            pe.wait_ge(xT_dve, 1)
            pe.wait_ge(xT_act, 1)
            project(0, 0, range(0, 2))
            project(0, 1, range(0, 2))
            turn_block(2, 0)
            turn_block(2, 1)
            pe.wait_ge(xT_dve, 2)
            pe.wait_ge(xT_act, 2)
            project(0, 0, range(2, 4))
            project(0, 1, range(2, 4))
            pe.wait_ge(xT_dve, 3)
            pe.wait_ge(xT_act, 3)
            project(0, 0, range(4, KT))
            project(0, 1, range(4, KT))
            turn_block(3, 0)
            turn_block(3, 1)
            pe.wait_ge(posb_step, E2)
            pe.wait_ge(par_in, 16 * N_PAR)
            pe.transpose(bank_o[:, 0:N_VEC], ln_rows[:], ident[0:N_VEC, 0:N_VEC])
            pe.wait_ge(by_depth, 1)
            pe.transpose(bank_o[0:HD, N_VEC:N_VEC + 1], bp_row_dh[:], ident[0:1, 0:1]).then_inc(par_psum, 1)
            pe.wait_ge(cls_ready, E2)
            project_paths(0)
            turn_block(4, 0)
            turn_block(4, 1)
            project(1, 0)
            project(1, 1)
            turn_block(5, 0)
            turn_block(5, 1)
            project_paths(1)
            pe.wait_ge(mats_in, 16 * N_MATS)
            pe.wait_ge(consts, N_CONST)
            pe.wait_ge(xT_dve, 2 * C)
            pe.wait_ge(xT_act, 2 * C)
            values_and_paths(0)
            pe.wait_ge(q_first_in, 16)
            broadcast_paths(0, 0)
            project(2, 0)
            slot(0)
            project(2, 1)
            pe.wait_ge(q_parts_in, 16)
            slot(1, start=lambda: project_paths(2), middle=lambda: project(3, 0))
            slot(2, middle=lambda: project(3, 1))
            project_paths(3)
            pe.wait_ge(dequant, 2)
            pe.wait_ge(bias_step, 5)
            pe.wait_ge(bias_act, 3)
            pe.wait_ge(path_f_ready, CHUNKS)
            slot(3)
            pe.wait_ge(q_parts_in, 32)
            with pe.Fori(LOOP.start, LOOP.stop) as t:
                slot(t)
            for t in range(LOOP.stop, TILES):
                slot(t)
            last_t = TILES - 1
            hidden(last_t - 2, 0)
            weigh(last_t)
            hidden(last_t - 2, 1)
            turn_ctx(last_t)
            turn_normed(last_t - 1)
            feed_forward_output(last_t - 2, 0)
            output_product(last_t)
            hidden(last_t - 1, 0)
            feed_forward_output(last_t - 2, 1)
            hidden(last_t - 1, 1)
            feed_forward_output(last_t - 1, 0)
            turn_normed(last_t)
            hidden(last_t, 0)
            feed_forward_output(last_t - 1, 1)
            hidden(last_t, 1)
            feed_forward_output(last_t, 0)
            feed_forward_output(last_t, 1)

        @block.scalar
        def _(act):
            act.preload_act_table(ACT.Exp)
            for dst, src in (
                (pos_rows[:], pos.rearrange("o t d -> (o t) d")),
                (tok_rows[0:E2], tok_b.rearrange("(e p) -> e p", p=128)),
                (tok_rows[E2:N_VEC], cls_token.rearrange("o q (e p) -> (o q e) p", p=128)),
            ):
                act.dma_start(dst, src).then_inc(tok_par_in, 16)
            for dst, src in (
                (bp_row[:], bp.rearrange("(o n) -> o n", o=1)),
                (wp_dh[:], Wp.rearrange("(e p) n -> p e n", p=128)),
                (ln_rows[0:E2], ln_gamma.rearrange("(e p) -> e p", p=128)),
                (ln_rows[E2:N_VEC], ln_beta.rearrange("(e p) -> e p", p=128)),
            ):
                act.dma_start(dst, src).then_inc(par_in, 16)

            for j, bank in enumerate((bank_y, bank_z, bank_v)):
                act.wait_ge(wT_psum, j + 1)
                act.activation(wT[:, 2 * j:2 * j + 2, :], bank[:].rearrange("p (k d) -> p k d", k=2),
                               ACT.Copy).then_inc(wT_ready, 1)

            def x_columns(n):
                act.wait_ge(xT_psum, 2 * n + 2)
                half, c = divmod(n, C)
                dst = xT[:, 2 * c + 1, half * HR * GRID:(half + 1) * HR * GRID].rearrange("p (r a g) -> p a g r", a=2, g=3)
                src = bank_cd[:, :, 0:3 * HR].rearrange("p a (g r) -> p a g r", g=3)
                act.activation(dst, src, ACT.Copy).then_inc(xT_act, 1)

            def paths(c):
                act.wait_ge(path_psum, c + 1)
                if c > 0:
                    act.wait_ge(split_step, 3 * c - 2)
                act.activation(path_f[:], bank_y[0:HD, 0:CT], ACT.Tanh, scale=0.5, bias=bp_half[:]).then_inc(path_f_ready, 1)
                act.wait_ge(path_f_ready, c + 1)
                if c >= 2:
                    act.wait_ge(path_out[c - 2], 16 * PARTS)
                act.activation(path_parts[:, c % 2, 0, :], path_f[:], ACT.Copy, scale=0.5).then_inc(path_hi_ready, 1)

            def own_paths(t):
                n = rows(t)
                act.wait_ge(proj_done, t + 1)
                if counts(t):
                    act.wait_ge(uB_done, t)
                act.activation(path_k[0:n, :], bank_v[0:n, D:D + HD], ACT.Tanh, scale=0.5).then_inc(path_k_ready, 1)

            def agreements(t):
                n = rows(t)
                act.wait_ge(uA_done, t + 1)
                act.activation(agree[0:n, H:2 * BR, :], agree[0:n, H:2 * BR, :], ACT.Copy, bias=0.5).then_inc(gA_done, 1)
                act.wait_ge(uB_done, t + 1)
                act.activation(agree[0:n, 2 * BR:4 * H, :], agree[0:n, 2 * BR:4 * H, :], ACT.Copy,
                               bias=0.5).then_inc(gB_done, 1)

            def values(t):
                n = rows(t)
                act.wait_ge(proj_done, t + 1)
                if counts(t):
                    act.wait_ge(pv_done, t)
                act.activation(v_ones[0:n, :, 0:DH], bank_v[0:n, 0:D].rearrange("p (h d) -> p h d", h=H),
                               ACT.Copy).then_inc(v_ready, 1)

            def exponentials(t):
                n = rows(t)
                act.wait_ge(sim_ready, t + 1)
                if counts(t):
                    act.wait_ge(pv_done, t)
                for b in range(images(t)):
                    last = act.activation(probs[0:n, :, b, :], sim[0:n], ACT.Exp, scale=1.0 / DEPTH,
                                          bias=own_image[0:n, b:b + 1])
                last.then_inc(probs_ready, 1)

            def ctx_columns(t):
                n = rows(t)
                act.wait_ge(ctxT_psum, t + 1)
                if counts(t):
                    act.wait_ge(n2T_psum, t)
                    act.wait_ge(wo_done, t)
                act.activation(ctxT[:, :, 0:n], bank_turn[:, 0:E2 * R].rearrange("p (e r) -> p e r", e=E2)[:, :, 0:n],
                               ACT.Copy).then_inc(ctxT_ready, 1)

            def normed_columns(t):
                n = rows(t)
                act.wait_ge(n2T_psum, t + 1)
                for e in range(E2):
                    last = act.activation(hnT[:, e, bass.ds(t * R, n)], bank_turn[:, (E2 + e) * R:(E2 + e) * R + n], ACT.Identity,
                                          scale=gamma_col[:, e:e + 1], bias=beta_col[:, e:e + 1])
                last.then_inc(hnT_ready, 1)

            def half_tanh(t, q):
                n = rows(t)
                act.wait_ge(y_psum, 2 * t + q + 1)
                act.activation(th[:, q, :, 0:n], bank_y[:, 0:FQ * R].rearrange("p (f n) -> p f n", f=FQ)[:, :, 0:n],
                               ACT.Tanh, scale=0.5).then_inc(th_ready, 1)

            def slot(t, start=None):
                if there(t):
                    agreements(t)
                if start:
                    start()
                if there(t - 3):
                    half_tanh(t - 3, 0)
                if there(t):
                    values(t)
                    exponentials(t)
                if there(t - 3):
                    half_tanh(t - 3, 1)
                if there(t - 1):
                    ctx_columns(t - 1)
                if there(t - 2):
                    normed_columns(t - 2)
                if there(t + 1):
                    own_paths(t + 1)

            for n in range(4):
                x_columns(n)
            act.wait_ge(colwise, 2)
            paths(0)
            x_columns(4)
            act.wait_ge(bias_in, 2 * PARTS * 16)
            act.activation(bias_parts[:], bias_f, ACT.Copy).then_inc(bias_act, 1)
            x_columns(5)
            paths(1)
            act.wait_ge(bias_step, 4)
            act.activation(bias_mid[:], bias_rest, ACT.Copy).then_inc(bias_act, 1)
            act.activation(bias_parts[32:64], bias_rest[32:64], ACT.Copy).then_inc(bias_act, 1)
            act.wait_ge(consts, N_CONST)
            slot(-1)
            slot(0)
            slot(1, start=lambda: paths(2))
            act.wait_ge(s2_in, 16)
            act.activation(s2[:], s2[:], ACT.Copy, scale=0.25).then_inc(s2_ready, 1)
            slot(2)
            paths(3)
            slot(3)
            with act.Fori(LOOP.start, LOOP.stop) as t:
                slot(t)
            for t in range(LOOP.stop, TILES + 3):
                slot(t)

        @block.vector
        def _(dve):
            tt, ts, stt = dve.tensor_tensor, dve.tensor_scalar, dve.scalar_tensor_tensor
            def by_patch(n):
                dve.wait_ge(x_in[n], 16)
                if n >= 2:
                    dve.wait_ge(xT_psum, 2 * n - 2)
                dve.tensor_copy(x_pat[:, n % 2].rearrange("p g (i j) -> p g i j", i=PATCH),
                                x_rows[:, n, :].rearrange("p (i g j) -> p g i j", i=PATCH, g=GRID)).then_inc(x_pat_ready, 1)

            def x_columns(n):
                dve.wait_ge(xT_psum, 2 * n + 1)
                half, c = divmod(n, C)
                dst = xT[:, 2 * c, half * HR * GRID:(half + 1) * HR * GRID].rearrange("p (r a g) -> p a g r", a=2, g=3)
                src = bank_bc[:, :, 0:3 * HR].rearrange("p a (g r) -> p a g r", g=3)
                dve.tensor_copy(dst, src).then_inc(xT_dve, 1)

            def tokens(c, e):
                dve.wait_ge(tok_psum, E2 * c + e + 1)
                tt(image_rows(hT[:, e, c * CT:(c + 1) * CT], T)[:, :, 1:T], image_rows((bank_y, bank_z)[e][:, 0:CP], NP),
                   spread(posb[:, e, 1:T], CI), ALU.add).then_inc(hT_ready, 1)

            def split_paths(c):
                dve.wait_ge(path_hi_ready, c + 1)
                if c > 0:
                    dve.wait_ge(split_step, 3 * c)
                stt(out=path_rest[:], in0=path_f[:], scalar=0.5, in1=path_parts[:, c % 2, 0, :], op0=ALU.mult,
                    op1=ALU.subtract).then_inc(split_step, 1)
                dve.wait_ge(split_step, 3 * c + 1)
                dve.tensor_copy(path_parts[:, c % 2, 1, :], path_rest[:]).then_inc(split_step, 1)
                dve.wait_ge(split_step, 3 * c + 2)
                tt(path_parts[:, c % 2, 2, :], path_rest[:], path_parts[:, c % 2, 1, :], ALU.subtract).then_inc(split_step, 1)

            def products(t, second):
                n = rows(t)
                if second:
                    dve.wait_ge(bcB_done, t + 1)
                else:
                    dve.wait_ge(bcA_done, t + 1)
                    dve.wait_ge(path_k_ready, t + 1)
                r = slice(second * 2 * BR, (second + 1) * 2 * BR)
                tt(agree[0:n, r, :].rearrange("p (k r) q -> p k r q", k=2),
                   bank_bc[0:n, :, 0:BR * T].rearrange("p k (r q) -> p k r q", q=T),
                   path_k[0:n, r].rearrange("p (k r o) -> p k r o", k=2, o=1).broadcast_to([n, 2, BR, T]),
                   ALU.mult).then_inc(uB_done if second else uA_done, 1)

            def depth(t, j):
                return agree[0:rows(t), j * H:(j + 1) * H, :].rearrange("p h q -> p (h q)")

            def inner_similarities(t):
                n = rows(t)
                dve.wait_ge(gA_done, t + 1)
                stt(out=horner[0:n, 0, :], in0=depth(t, 0), scalar=1.5, in1=depth(t, 1), op0=ALU.add,
                    op1=ALU.mult).then_inc(horner_step, 1)
                dve.wait_ge(gB_done, t + 1)
                dve.wait_ge(horner_step, 3 * t + 1)
                stt(out=horner[0:n, 1, :], in0=horner[0:n, 0, :], scalar=1.0, in1=depth(t, 2), op0=ALU.add,
                    op1=ALU.mult).then_inc(horner_step, 1)

            def outer_similarities(t):
                n = rows(t)
                dve.wait_ge(horner_step, 3 * t + 2)
                stt(out=horner[0:n, 0, :], in0=horner[0:n, 1, :], scalar=1.0, in1=depth(t, 3), op0=ALU.add,
                    op1=ALU.mult).then_inc(horner_step, 1)
                dve.wait_ge(g0_done, t + 1)
                dve.wait_ge(horner_step, 3 * t + 3)
                if counts(t):
                    dve.wait_ge(probs_ready, t)
                stt(out=sim[0:n].rearrange("p h q -> p (h q)"), in0=horner[0:n, 0, :], scalar=1.0, in1=depth(t, 4),
                    op0=ALU.add, op1=ALU.mult).then_inc(sim_ready, 1)

            def normalise_ctx(t):
                n = rows(t)
                weighted = bank_ctx[0:n, 0:H * (DH + 1)].rearrange("p (h d) -> p h d", h=H)
                dve.wait_ge(pv_done, t + 1)
                dve.reciprocal(recip[0:n, :], weighted[:, :, DH]).then_inc(recip_done, 1)
                dve.wait_ge(recip_done, t + 1)
                if counts(t):
                    dve.wait_ge(ctxT_psum, t)
                tt(ctx_rows[0:n, :].rearrange("p (h d) -> p h d", h=H), weighted[:, :, 0:DH],
                   recip[0:n, :].rearrange("p (h o) -> p h o", o=1).broadcast_to([n, H, DH]), ALU.mult).then_inc(ctx_ready, 1)

            def measure(t):
                n = rows(t)
                dve.wait_ge(wo_done, t + 1)
                dve.bn_stats(stats[0:n, :], bank_o[0:n, 0:D])
                dve.drain()
                dve.bn_aggr(mv[0:n, :], stats[0:n, :]).then_inc(mv_ready, 1)

            def normalise(t):
                n = rows(t)
                dve.wait_ge(rstd_ready, t + 1)
                row = h2[0:n, bass.ds(t, 1), :].rearrange("p o d -> p (o d)")
                ts(row, bank_o[0:n, 0:D], mv[0:n, 0:1], rstd[0:n, 0:1], ALU.subtract, ALU.mult).then_inc(h2_ready, 1)
                dve.wait_ge(h2_ready, t + 1)
                if counts(t):
                    dve.wait_ge(n2T_psum, t)
                ts(n2[0:n, :], row, rstd[0:n, 1:2], None, ALU.mult).then_inc(n2_ready, 1)

            def silu(t, q):
                n = rows(t)
                dve.wait_ge(th_ready, 2 * t + q + 1)
                if counts(t):
                    dve.wait_ge(z_psum, 2 * t + q - 1)
                stt(out=act2[:, q * FQ:(q + 1) * FQ, 0:n], in0=th[:, q, :, 0:n], scalar=1.0,
                    in1=bank_y[:, 0:FQ * R].rearrange("p (f n) -> p f n", f=FQ)[:, :, 0:n], op0=ALU.add,
                    op1=ALU.mult).then_inc(act_ready, 1)

            def residual(t):
                n = rows(t)
                dve.wait_ge(z_psum, 2 * t + 2)
                if counts(t):
                    dve.wait_ge(fin_ready, t)
                row = h2[0:n, bass.ds(t, 1), :].rearrange("p o d -> p (o d)")
                stt(out=res[0:n, :], in0=row, scalar=2.0, in1=bank_z[0:n, 0:D], op0=ALU.mult,
                    op1=ALU.add).then_inc(res_ready, 1)
                dve.wait_ge(res_ready, t + 1)
                dve.bn_stats(fstats[0:n, :], res[0:n, :])
                dve.drain()
                dve.bn_aggr(fmv[0:n, :], fstats[0:n, :]).then_inc(fmv_ready, 1)

            def final(t):
                n = rows(t)
                dve.wait_ge(frstd_ready, t + 1)
                if counts(t):
                    dve.wait_ge(stored, 16 * t)
                ts(fin[0:n, :], res[0:n, :], fmv[0:n, 0:1], frstd[0:n, 0:1], ALU.subtract, ALU.mult).then_inc(fin_ready, 1)

            def slot(t, middle=None):
                if there(t):
                    products(t, 1)
                if there(t - 2):
                    measure(t - 2)
                if there(t):
                    inner_similarities(t)
                if there(t - 3):
                    silu(t - 3, 0)
                if there(t):
                    outer_similarities(t)
                if there(t - 1):
                    normalise_ctx(t - 1)
                if there(t - 2):
                    normalise(t - 2)
                if middle:
                    middle()
                if there(t - 4):
                    residual(t - 4)
                if there(t - 3):
                    silu(t - 3, 1)
                if there(t - 4):
                    final(t - 4)
                if there(t + 1):
                    products(t + 1, 0)

            by_patch(0)
            by_patch(1)
            x_columns(0)
            by_patch(2)
            dve.wait_ge(pos_psum, 1)
            dve.tensor_copy(tok_cols[:], bank_o[:, E2 * T:E2 * T + N_VEC]).then_inc(tok_cols_ready, 1)
            dve.wait_ge(tok_cols_ready, 1)
            for e in range(E2):
                ts(posb[:, e, 1:T], bank_o[:, e * T + 1:(e + 1) * T], tokb_col[:, e:e + 1], None, ALU.add)
                tt(posb[:, e, 0:1], bank_o[:, e * T:e * T + 1], cls_col[:, e:e + 1], ALU.add).then_inc(posb_step, 1)
            x_columns(1)
            dve.wait_ge(posb_step, E2)
            for e in range(E2):
                dve.tensor_copy(image_rows(hT[:, e, :], T)[:, :, 0], posb[:, e, 0:1].broadcast_to([128, B])).then_inc(cls_ready, 1)
            x_columns(2)
            by_patch(3)
            dve.wait_ge(par_in, 16 * N_PAR)
            for j in range(DEPTH):
                d = DEPTH - 1 - j
                dve.tensor_copy(bp_row_dh[:, j * H:(j + 1) * H], bp_row[:].rearrange("o (h d) -> o h d", d=DEPTH)[:, :, d])
                last = dve.tensor_copy(wvp[:, :, D + j * H:D + (j + 1) * H],
                                       wp_dh[:].rearrange("p e (h d) -> p e h d", d=DEPTH)[:, :, :, d])
            last.then_inc(by_depth, 1)
            tokens(0, 0)
            tokens(0, 1)
            dve.wait_ge(par_psum, 1)
            dve.tensor_copy(ln_cols[:], bank_o[:, 0:N_VEC]).then_inc(colwise, 1)
            ts(bp_half[:], bank_o[0:HD, N_VEC:N_VEC + 1], 0.5, None, ALU.mult).then_inc(colwise, 1)
            x_columns(3)
            by_patch(4)
            by_patch(5)
            split_paths(0)
            x_columns(4)
            dve.wait_ge(q1_in, 32)
            stt(out=w1[:], in0=q1[:], scalar=-ZERO_POINT, in1=s1[:], op0=ALU.add, op1=ALU.mult).then_inc(dequant, 1)
            tokens(1, 0)
            tokens(1, 1)
            x_columns(5)
            split_paths(1)
            slot(-1)
            tokens(2, 0)
            slot(0)
            tokens(2, 1)

            def split_and_tokens():
                split_paths(2)
                tokens(3, 0)

            slot(1, middle=split_and_tokens)
            slot(2, middle=lambda: tokens(3, 1))
            dve.wait_ge(q2_in, 16)
            dve.wait_ge(s2_ready, 1)
            dve.wait_ge(bias_step, 5)
            stt(out=w2[:], in0=q2[:], scalar=-ZERO_POINT, in1=s2[:], op0=ALU.add, op1=ALU.mult).then_inc(dequant, 1)
            slot(3, middle=lambda: split_paths(3))
            with dve.Fori(LOOP.start, LOOP.stop) as t:
                slot(t)
            for t in range(LOOP.stop, TILES + 4):
                slot(t)


_INS = ["x", "L0_tok_W", "L0_tok_b", "L0_tok_cls_token", "L0_tok_pos_embedding", "L0_attn_Wp", "L0_attn_bp",
        "L0_attn_Wv", "L0_attn_Wo", "L0_ffn_ln_gamma", "L0_ffn_ln_beta", "L0_ffn_fc1_q", "L0_ffn_fc1_scales",
        "L0_ffn_fc1_bias", "L0_ffn_fc2_q", "L0_ffn_fc2_scales", "L0_ffn_fc2_bias"]


def kernel(**inputs):
    import numpy as np
    import concourse.bacc as bacc
    from concourse.bass_utils import run_bass_kernel_spmd

    nc = bacc.Bacc("TRN2", target_bir_lowering=False, num_devices=1)
    arrays, args = {}, []
    for name in _INS:
        a = np.ascontiguousarray(inputs[name])
        arrays[f"in_{name}"] = a
        args.append(nc.dram_tensor(f"in_{name}", a.shape, mybir.dt.from_np(a.dtype), kind="ExternalInput").ap())
    B = inputs["x"].shape[0]
    _, T, D = inputs["L0_tok_pos_embedding"].shape
    args.append(nc.dram_tensor("out_0", (B, T, D), F32, kind="ExternalOutput").ap())
    vit_block(nc, *args)
    r = run_bass_kernel_spmd(nc, [arrays], core_ids=[0])
    return r.results[0]["out_0"]
```

```python
from contextlib import ExitStack

import concourse.bass as bass
from concourse import mybir

ALU = mybir.AluOpType
ACT = mybir.ActivationFunctionType
F32 = mybir.dt.float32
BF16 = mybir.dt.bfloat16
I32 = mybir.dt.int32
EPS = 1e-5
MASKED = -1e4
ZERO_POINT = 128.0


def vit_block(nc, x, tok_W, tok_b, cls_token, pos, Wp, bp, Wv, Wo, ln_gamma, ln_beta,
              fc1_q, fc1_scales, fc1_bias, fc2_q, fc2_scales, fc2_bias, out):
    B, C, IMG, _ = x.shape
    D, PATCH_DIM = tok_W.shape
    T = pos.shape[1]
    NP = T - 1
    PATCH = 16
    GRID = IMG // PATCH
    KT = PATCH_DIM // 128
    E2 = D // 128
    HALF = B // 2
    HR = HALF * GRID
    HD = Wp.shape[1]
    H = 8
    DEPTH = HD // H
    DH = D // H
    NTOK = B * T
    IT = 3
    R = IT * T
    TILES = -(-B // IT)
    CI = 8
    CHUNKS = B // CI
    CP, CT = CI * NP, CI * T
    F = fc1_q.shape[1]
    FB = F // 128
    FQ = FB // 2
    G1, G2 = fc1_scales.shape[0], fc2_scales.shape[0]
    UROWS = HD * T
    PARTS = 3
    WARM_UP = 17

    def images(t):
        return min(IT, B - t * IT) if isinstance(t, int) else IT

    def rows(t):
        return images(t) * T

    def there(t):
        return not isinstance(t, int) or 0 <= t < TILES

    def counts(n):
        return not isinstance(n, int) or n > 0

    with ExitStack() as ctx:
        def sb(name, shape, dt=F32):
            return ctx.enter_context(nc.sbuf_tensor(name, shape, dt))

        def ps(name, shape):
            return ctx.enter_context(nc.psum_tensor(name, shape, F32))

        def sem(name):
            return ctx.enter_context(nc.semaphore(name))

        bank_y = ps("bank_y", [128, 2, 512])
        bank_cd = ps("bank_cd", [128, 2, 512])
        bank_ctx, bank_turn = bank_cd[:, 0, :], bank_cd[:, 1, :]
        weighted, weights = (bank_ctx[:, i * E2 * R:(i + 1) * E2 * R].rearrange("p (g n) -> p g n", g=E2)
                             for i in range(2))
        bank_t = ps("bank_t", [128, 512])
        bank_z = ps("bank_z", [128, 512])
        bank_v = ps("bank_v", [128, 512])
        bank_o = ps("bank_o", [128, 512])

        ident = sb("ident", [128, 128])
        x_rows_all = sb("x_rows", [128, 2 * C * PATCH * IMG])
        x_rows = x_rows_all[0:HR, :].rearrange("p (n k) -> p n k", n=2 * C)
        xT = sb("xT", [128, KT, B * NP])
        w_rows = sb("w_rows", [128, E2, PATCH_DIM])
        wT = sb("wT", [128, KT, D])
        pos_rows = sb("pos_rows", [T, D])
        N_VEC = 2 * E2
        tok_rows = sb("tok_rows", [N_VEC, 128])
        tok_cols = sb("tok_cols", [128, N_VEC])
        tokb_col, cls_col = tok_cols[:, 0:E2], tok_cols[:, E2:N_VEC]
        ln_rows = sb("ln_rows", [N_VEC, 128])
        ln_cols = sb("ln_cols", [128, N_VEC])
        gamma_col, beta_col = ln_cols[:, 0:E2], ln_cols[:, E2:N_VEC]
        posb = sb("posb", [128, E2, T])
        hT = sb("hT", [128, E2, NTOK])
        hT_proj = sb("hT_proj", [128, E2, R])
        hT_res = sb("hT_res", [128, E2, R])
        wvp = sb("wvp", [128, E2, D + HD])
        wp_dh = sb("wp_dh", [128, E2, HD])
        bp_half = sb("bp_half", [HD, 1])
        bp_row = sb("bp_row", [1, HD])
        bp_row_dh = sb("bp_row_dh", [1, HD])
        path_f = sb("path_f", [HD, NTOK])
        path_rest = sb("path_rest", [HD, CT])
        path_parts = sb("path_parts", [HD, PARTS, NTOK], BF16)
        ident_bf = sb("ident_bf", [HD, HD], BF16)
        path_q = sb("path_q", [128, UROWS])
        path_k = sb("path_k", [128, HD])
        agree = sb("agree", [128, HD, T])
        causal = sb("causal", [128, T])
        own_image = sb("own_image", [128, IT])
        horner = sb("horner", [128, 2, H * T])
        sim = sb("sim", [128, H, T])
        probs = sb("probs", [128, H, IT, T])
        v_rows = sb("v_rows", [128, D])
        ones_sum = sb("ones_sum", [128, DH])
        recip = sb("recip", [128, E2, R])
        ctxT = sb("ctxT", [128, E2, R])
        wo = sb("wo", [128, E2, D])
        stats = sb("stats", [128, 6])
        mv = sb("mv", [128, 2])
        small = sb("small", [128, 4])
        rstd = sb("rstd", [128, 2])
        minus_half = sb("minus_half", [128, 1])
        eps_col = sb("eps_col", [128, 1])
        assert TILES * D <= 2 * PATCH * IMG
        patches = sb("patches", [128, 2 * PATCH * IMG])
        x_pat = patches[0:HR, :].rearrange("p (n g k) -> p n g k", n=2, g=GRID)
        h2 = patches[:, 0:TILES * D].rearrange("p (t d) -> p t d", t=TILES)
        n2 = sb("n2", [128, D])
        hnT = sb("hnT", [128, E2, NTOK])
        q1 = sb("q1", [128, G1, F], I32)
        q2 = sb("q2", [128, G2, D], I32)
        s1 = sb("s1", [128, G1, F])
        s2 = sb("s2", [128, G2, D])
        w1 = sb("w1", [128, G1, F])
        w2 = sb("w2", [128, G2, D])
        BIAS = 32 * PARTS
        bias_f = sb("bias_f", [BIAS, 2, 128])
        bias_rest = sb("bias_rest", [BIAS, 2, 128])
        bias_mid = sb("bias_mid", [BIAS, 2, 128], BF16)
        bias_parts = sb("bias_parts", [BIAS, 2, 128], BF16)
        own_block = sb("own_block", [BIAS, FQ, R], BF16)
        b2_quarter = sb("b2_quarter", [128, D])
        th = x_rows_all[:, 0:FB * R].rearrange("p (q f n) -> p q f n", q=2, f=FQ)
        act2 = x_rows_all[:, FB * R:2 * FB * R].rearrange("p (f n) -> p f n", f=FB)
        res = sb("res", [128, D])
        fstats = sb("fstats", [128, 6])
        fmv = sb("fmv", [128, 2])
        fvar = sb("fvar", [128, 1])
        frstd = sb("frstd", [128, 1])
        fin = sb("fin", [128, D])

        path_dram = nc.dram_tensor("path_dram", (B, HD, T), F32, kind="Internal").ap()

        w_in = sem("w_in")
        x_in = [sem(f"x_in{i}") for i in range(2 * C)]
        tok_par_in = sem("tok_par_in")
        par_in = sem("par_in")
        mats_in = sem("mats_in")
        q1_in = sem("q1_in")
        q2_in = sem("q2_in")
        s2_in = sem("s2_in")
        bias_in = sem("bias_in")
        consts = sem("consts")
        bias_step = sem("bias_step")
        b2_in = sem("b2_in")
        b2_ready = sem("b2_ready")
        carry_ready = sem("carry_ready")
        by_depth = sem("by_depth")
        tok_cols_ready = sem("tok_cols_ready")
        colwise = sem("colwise")
        wT_psum = sem("wT_psum")
        wT_ready = sem("wT_ready")
        pos_psum = sem("pos_psum")
        par_psum = sem("par_psum")
        posb_step = sem("posb_step")
        x_pat_ready = sem("x_pat_ready")
        xT_psum = sem("xT_psum")
        xT_dve = sem("xT_dve")
        xT_act = sem("xT_act")
        tok_psum = sem("tok_psum")
        hT_ready = sem("hT_ready")
        cls_ready = sem("cls_ready")
        path_psum = sem("path_psum")
        path_f_ready = sem("path_f_ready")
        path_hi_ready = sem("path_hi_ready")
        split_step = sem("split_step")
        path_out = [sem(f"path_out{c}") for c in range(CHUNKS)]
        path_q_in = sem("path_q_in")
        s2_ready = sem("s2_ready")
        dequant = sem("dequant")
        hT_proj_in = sem("hT_proj_in")
        hT_res_in = sem("hT_res_in")
        proj_done = sem("proj_done")
        path_k_ready = sem("path_k_ready")
        v_ready = sem("v_ready")
        u_done = sem("u_done")
        g_done = sem("g_done")
        g0_done = sem("g0_done")
        horner_step = sem("horner_step")
        sim_ready = sem("sim_ready")
        probs_ready = sem("probs_ready")
        pv_done = sem("pv_done")
        recip_done = sem("recip_done")
        ctxT_ready = sem("ctxT_ready")
        wo_done = sem("wo_done")
        mv_ready = sem("mv_ready")
        rstd_step = sem("rstd_step")
        rstd_ready = sem("rstd_ready")
        h2_ready = sem("h2_ready")
        n2_ready = sem("n2_ready")
        n2T_psum = sem("n2T_psum")
        hnT_ready = sem("hnT_ready")
        y_psum = sem("y_psum")
        th_ready = sem("th_ready")
        act_ready = sem("act_ready")
        z_psum = sem("z_psum")
        res_ready = sem("res_ready")
        fmv_ready = sem("fmv_ready")
        frstd_step = sem("frstd_step")
        frstd_ready = sem("frstd_ready")
        fin_ready = sem("fin_ready")
        stored = sem("stored")

        N_CONST = 14
        N_TOK_PAR, N_PAR, N_MATS = 3, 4, 2
        LOOP = range(3, TILES - 2)
        out_flat = out.rearrange("b t d -> (b t) d")


        def path_bank(c):
            return bank_o if c == 1 else bank_t

        def output_bank(t):
            return bank_t if isinstance(t, int) and t == TILES - 1 else bank_z

        def image_rows(ap, n):
            return ap.rearrange("p (b t) -> p b t", t=n)

        def spread(ap, n):
            return ap.rearrange("p (o t) -> p o t", o=1).broadcast_to([ap.shape[0], n, ap.shape[1]])

        block = ctx.enter_context(nc.Block())

        @block.sync
        def _(sp):
            sp.dma_start(w_rows[:], tok_W.rearrange("(e p) k -> p e k", p=128)).then_inc(w_in, 16)
            for half in range(2):
                for c in range(C):
                    n = half * C + c
                    src = x[half * HALF:(half + 1) * HALF, c].rearrange("b (g i) w -> b g (i w)", i=PATCH)
                    sp.dma_start(x_rows[:, n, :], src).then_inc(x_in[n], 16)
            for dst, src in (
                (bp_row[:], bp.rearrange("(o n) -> o n", o=1)),
                (wp_dh[:], Wp.rearrange("(e p) n -> p e n", p=128)),
                (ln_rows[0:E2], ln_gamma.rearrange("(e p) -> e p", p=128)),
                (ln_rows[E2:N_VEC], ln_beta.rearrange("(e p) -> e p", p=128)),
            ):
                sp.dma_start(dst, src).then_inc(par_in, 16)
            sp.dma_start(wvp[:, :, 0:D], Wv.rearrange("(e p) n -> p e n", p=128)).then_inc(mats_in, 16)
            sp.dma_start(wo[:], Wo.rearrange("(e p) n -> p e n", p=128)).then_inc(mats_in, 16)
            sp.dma_start(q1[:], fc1_q.rearrange("(g p) n -> p g n", p=128)).then_inc(q1_in, 16)
            sp.dma_start(s1[:], fc1_scales.rearrange("(o g) n -> o g n", o=1).broadcast_to([128, G1, F])).then_inc(q1_in, 16)
            sp.wait_ge(bias_step, 1)
            for part in range(PARTS):
                sp.dma_start(bias_f[32 * part:32 * part + FQ],
                             fc1_bias.rearrange("(q i p) -> i q p", i=FQ, p=128)).then_inc(bias_in, 16)
            sp.dma_start(b2_quarter[:], fc2_bias.rearrange("(o n) -> o n", o=1).broadcast_to([128, D])).then_inc(b2_in, 16)


            def paths_out(c):
                sp.wait_ge(path_f_ready, c + 1)
                sp.dma_start(path_dram[c * CI:(c + 1) * CI].rearrange("b r t -> r b t"),
                             image_rows(path_f[:, c * CT:(c + 1) * CT], T)).then_inc(path_out[c], 16)

            def load_path_q(t):
                if isinstance(t, int):
                    sp.wait_ge(path_out[((t + 1) * IT - 1) // CI if t < TILES - 1 else CHUNKS - 1], 16)
                if counts(t):
                    sp.wait_ge(u_done, t)
                for i in range(images(t)):
                    src = path_dram[bass.ds(t * IT + i, 1)].rearrange("b r t -> b (r t)")
                    sp.dma_start(path_q[i * T:(i + 1) * T, :], src.broadcast_to([T, UROWS])).then_inc(path_q_in, 16)

            def load_proj(t):
                if counts(t):
                    sp.wait_ge(proj_done, t)
                sp.dma_start(hT_proj[:, :, 0:rows(t)],
                             hT[:, :, bass.ds(t * R, rows(t))]).then_inc(hT_proj_in, 16)

            def load_res(t):
                if counts(t):
                    sp.wait_ge(wo_done, t)
                sp.dma_start(hT_res[:, :, 0:rows(t)],
                             hT[:, :, bass.ds(t * R, rows(t))]).then_inc(hT_res_in, 16)

            def store(t):
                n = rows(t)
                sp.wait_ge(fin_ready, t + 1)
                sp.dma_start(out_flat[bass.ds(t * R, n), :], fin[0:n, :]).then_inc(stored, 16)

            def slot(t):
                if there(t + 1):
                    load_path_q(t + 1)
                if there(t + 2):
                    load_proj(t + 2)
                if there(t):
                    load_res(t)
                if there(t - 3):
                    store(t - 3)

            sp.wait_ge(hT_ready, E2)
            sp.wait_ge(cls_ready, E2)
            load_proj(0)
            paths_out(0)
            load_path_q(0)
            load_proj(1)
            load_res(0)
            sp.dma_start(q2[:], fc2_q.rearrange("(g p) n -> p g n", p=128)).then_inc(q2_in, 16)
            load_path_q(1)
            paths_out(1)
            sp.wait_ge(hT_ready, E2 * CHUNKS // 2)
            load_proj(2)
            sp.dma_start(s2[:], fc2_scales.rearrange("(o g) n -> o g n", o=1).broadcast_to([128, G2, D])).then_inc(s2_in, 16)
            slot(1)
            paths_out(2)
            slot(2)
            paths_out(3)
            sp.wait_ge(hT_ready, E2 * CHUNKS)
            for c in range(CHUNKS):
                sp.wait_ge(path_out[c], 16)
            with sp.Fori(LOOP.start, LOOP.stop - 1) as t:
                slot(t)
            for t in range(LOOP.stop - 1, TILES + 3):
                slot(t)
            sp.wait_ge(stored, 16 * TILES)

        @block.gpsimd
        def _(pool):
            def const(ins):
                ins.then_inc(consts, 1)

            const(pool.memset(ident[:], 1.0))
            pool.wait_ge(consts, 1)
            const(pool.affine_select(out=ident[:], in_=ident[:], compare_op=ALU.is_equal, fill=0.0, base=0,
                                     pattern=[[-1, 128]], channel_multiplier=1))
            const(pool.memset(minus_half[:], -0.5))
            const(pool.memset(eps_col[:], EPS))
            const(pool.memset(ones_sum[:], 1.0))
            const(pool.memset(ident_bf[:], 0.0))
            const(pool.memset(own_image[:], 0.0))
            const(pool.memset(causal[:], 0.5))
            pool.wait_ge(consts, 8)
            const(pool.affine_select(out=ident_bf[:], in_=ident_bf[:], compare_op=ALU.not_equal, fill=1.0, base=0,
                                     pattern=[[-1, HD]], channel_multiplier=1))
            pool.wait_ge(consts, 9)
            const(pool.affine_select(out=own_image[:], in_=own_image[:], compare_op=ALU.is_ge, fill=MASKED, base=0,
                                     pattern=[[-T, IT]], channel_multiplier=1))
            pool.wait_ge(consts, 10)
            const(pool.affine_select(out=own_image[:], in_=own_image[:], compare_op=ALU.is_ge, fill=MASKED,
                                     base=T - 1, pattern=[[T, IT]], channel_multiplier=-1))
            pool.wait_ge(consts, 11)
            for b in reversed(range(IT)):
                const(pool.affine_select(out=causal[0:T * (b + 1)], in_=causal[0:T * (b + 1)], compare_op=ALU.is_ge,
                                         fill=MASKED, base=T * b, pattern=[[1, T]], channel_multiplier=-1))
                pool.wait_ge(consts, 11 + IT - b)

            def bias_step_done(ins):
                ins.then_inc(bias_step, 1)

            bias_step_done(pool.memset(bias_f[:], 0.0))
            bias_step_done(pool.memset(own_block[:], 0.0))
            pool.wait_ge(bias_step, 2)
            for part in range(PARTS):
                some = own_block[32 * part:32 * (part + 1)]
                bias_step_done(pool.affine_select(out=some, in_=some, compare_op=ALU.not_equal, fill=1.0, base=0,
                                                  pattern=[[1, FQ], [0, R]], channel_multiplier=-1))
                pool.wait_ge(bias_step, 3 + part)
            pool.wait_ge(bias_in, PARTS * 16)
            bias_step_done(pool.tensor_copy(bias_parts[:], bias_f[:]))
            pool.wait_ge(bias_step, 6)
            bias_step_done(pool.tensor_tensor(bias_rest[:], bias_f[:], bias_parts[:], ALU.subtract))
            pool.wait_ge(bias_step, 7)
            bias_step_done(pool.tensor_copy(bias_mid[:], bias_rest[:]))
            pool.wait_ge(bias_step, 8)
            bias_step_done(pool.tensor_copy(bias_parts[32:64], bias_mid[32:64]))
            pool.wait_ge(bias_step, 9)
            bias_step_done(pool.tensor_tensor(bias_parts[64:96], bias_rest[64:96], bias_mid[64:96], ALU.subtract))
            pool.wait_ge(bias_step, 10)
            pool.wait_ge(b2_ready, 1)

            def last_agreement(t):
                n = rows(t)
                pool.wait_ge(u_done, t + 1)
                pool.tensor_tensor(agree[0:n, 4 * H:5 * H, :], agree[0:n, 4 * H:5 * H, :],
                                   spread(causal[0:n, :], H), ALU.add).then_inc(g0_done, 1)

            def norms(t):
                n = rows(t)
                pool.wait_ge(mv_ready, t + 1)
                steps = ((small[0:n, 0:1], mv[0:n, 1:2], eps_col[0:n], ALU.add),
                         (rstd[0:n, 0:1], small[0:n, 0:1], minus_half[0:n], ALU.pow),
                         (small[0:n, 1:2], rstd[0:n, 0:1], rstd[0:n, 0:1], ALU.mult),
                         (small[0:n, 2:3], small[0:n, 1:2], mv[0:n, 1:2], ALU.mult),
                         (small[0:n, 3:4], small[0:n, 2:3], eps_col[0:n], ALU.add))
                for i, (dst, a, b, op) in enumerate(steps):
                    pool.tensor_tensor(dst, a, b, op).then_inc(rstd_step, 1)
                    pool.wait_ge(rstd_step, len(steps) * t + i + 1)
                pool.tensor_tensor(rstd[0:n, 1:2], small[0:n, 3:4], minus_half[0:n], ALU.pow).then_inc(rstd_ready, 1)

            def carry(t):
                n = rows(t)
                row = h2[0:n, bass.ds(t, 1), :].rearrange("p o d -> p (o d)")
                pool.wait_ge(n2_ready, t + 1)
                pool.tensor_tensor(row, row, b2_quarter[0:n, :], ALU.add).then_inc(carry_ready, 1)

            def final_norm(t):
                n = rows(t)
                pool.wait_ge(fmv_ready, t + 1)
                pool.tensor_tensor(fvar[0:n], fmv[0:n, 1:2], eps_col[0:n], ALU.add).then_inc(frstd_step, 1)
                pool.wait_ge(frstd_step, t + 1)
                pool.tensor_tensor(frstd[0:n], fvar[0:n], minus_half[0:n], ALU.pow).then_inc(frstd_ready, 1)

            def slot(t):
                if there(t):
                    last_agreement(t)
                if there(t - 1):
                    norms(t - 1)
                if there(t - 3):
                    final_norm(t - 3)
                if there(t - 1):
                    carry(t - 1)

            for t in range(LOOP.start):
                slot(t)
            with pool.Fori(LOOP.start, LOOP.stop) as t:
                slot(t)
            for t in range(LOOP.stop, TILES + 3):
                slot(t)

        @block.tensor
        def _(pe):
            mm = pe.matmul
            pe.wait_ge(consts, 2)
            for _ in range(WARM_UP):
                pe.transpose(bank_v[:, 0:128], ident[:], ident[:])
            pe.wait_ge(w_in, 16)
            for j, bank in enumerate((bank_t, bank_z, bank_v)):
                for k in (2 * j, 2 * j + 1):
                    for e in range(E2):
                        at = (k % 2) * D + e * 128
                        last = pe.transpose(bank[:, at:at + 128], w_rows[:, e, k * 128:(k + 1) * 128], ident[:])
                last.then_inc(wT_psum, 1)

            def turn_block(n, ih):
                banks = (bank_y, bank_cd)[ih]
                pe.wait_ge(x_pat_ready, n + 1)
                if n > 0:
                    pe.wait_ge(xT_act if ih else xT_dve, n)
                for g in range(GRID):
                    last = pe.transpose(banks[:, g // 3, (g % 3) * HR:(g % 3 + 1) * HR],
                                        x_pat[:, n % 2, g, ih * 128:(ih + 1) * 128], ident[0:HR, 0:HR])
                last.then_inc(xT_psum, 1)

            def project(c, e, blocks=range(KT)):
                bank = (bank_t, bank_z)[e]
                if c > 0:
                    pe.wait_ge(hT_ready, E2 * (c - 1) + e + 1)
                    if e == 0 and c == 1:
                        pe.wait_ge(path_f_ready, c)
                for k in blocks:
                    last = mm(bank[:, 0:CP], wT[:, k, e * 128:(e + 1) * 128], xT[:, k, c * CP:(c + 1) * CP],
                              start=(k == 0), stop=(k == KT - 1))
                if KT - 1 in blocks:
                    last.then_inc(tok_psum, 1)

            def project_paths(c):
                pe.wait_ge(hT_ready, E2 * (c + 1) + (c == CHUNKS - 2))
                if c == 1:
                    pe.wait_ge(colwise, 2)
                if c == CHUNKS - 1:
                    pe.wait_ge(path_f_ready, c)
                for e in range(E2):
                    last = mm(path_bank(c)[0:HD, 0:CT], wvp[:, e, D:D + HD], hT[:, e, c * CT:(c + 1) * CT],
                              start=(e == 0), stop=(e == E2 - 1))
                last.then_inc(path_psum, 1)

            def values_and_paths(t):
                n = rows(t)
                pe.wait_ge(hT_proj_in, 16 * (t + 1))
                if counts(t):
                    pe.wait_ge(v_ready, t)
                    pe.wait_ge(path_k_ready, t)
                mm(bank_v[0:n, 0:D], hT_proj[:, 0, 0:n], wvp[:, 0, 0:D], start=True, stop=False)
                mm(bank_v[0:n, 0:D], hT_proj[:, 1, 0:n], wvp[:, 1, 0:D], start=False, stop=True)
                chunks = -(-min(B, (t + 1) * IT) // CI) if isinstance(t, int) else CHUNKS
                pe.wait_ge(split_step, 3 * chunks)
                for part in range(PARTS):
                    last = mm(bank_v[0:n, D:D + HD], path_parts[:, part, bass.ds(t * R, n)], ident_bf[:],
                              start=(part == 0), stop=(part == PARTS - 1))
                last.then_inc(proj_done, 1)

            def weigh(t):
                n = rows(t)
                pe.wait_ge(probs_ready, t + 1)
                pe.wait_ge(v_ready, t + 1)
                if counts(t):
                    pe.wait_ge(ctxT_ready, t)
                for block in range(E2):
                    for dst, values in ((weighted, v_rows), (weights, ones_sum)):
                        for i in range(128 // DH):
                            h = block * (128 // DH) + i
                            at = 0 if values is ones_sum else h * DH
                            last = mm(dst[i * DH:(i + 1) * DH, block, 0:n], values[0:n, at:at + DH],
                                      probs[0:n, h, 0:images(t), :].rearrange("p b q -> p (b q)"),
                                      start=True, stop=True)
                last.then_inc(pv_done, 1)

            def output_product(t):
                n = rows(t)
                pe.wait_ge(ctxT_ready, t + 1)
                pe.wait_ge(hT_res_in, 16 * (t + 1))
                if counts(t):
                    pe.wait_ge(h2_ready, t)
                else:
                    pe.wait_ge(path_f_ready, 2)
                mm(bank_o[0:n, 0:D], ctxT[:, 0, 0:n], wo[:, 0, :], start=True, stop=False)
                mm(bank_o[0:n, 0:D], ctxT[:, 1, 0:n], wo[:, 1, :], start=False, stop=False)
                mm(bank_o[0:n, 0:128], hT_res[:, 0, 0:n], ident[:], start=False, stop=False)
                mm(bank_o[0:n, 128:D], hT_res[:, 1, 0:n], ident[:], start=False, stop=True).then_inc(wo_done, 1)

            def turn_normed(t):
                n = rows(t)
                pe.wait_ge(n2_ready, t + 1)
                if counts(t):
                    pe.wait_ge(hnT_ready, t)
                for e in range(E2):
                    last = pe.transpose(bank_turn[:, e * R:e * R + n], n2[0:n, e * 128:(e + 1) * 128], ident[0:n, 0:n])
                last.then_inc(n2T_psum, 1)

            def hidden(t, q):
                n = rows(t)
                if q == 0:
                    pe.wait_ge(hnT_ready, t + 1)
                if counts(2 * t + q - 1):
                    pe.wait_ge(act_ready, 2 * t + q - 1)
                else:
                    pe.wait_ge(dequant, 1)
                    pe.wait_ge(bias_step, 10)
                blocks = bank_y[:, q, 0:FQ * R].rearrange("p (i n) -> p i n", i=FQ)
                mm(blocks[:, :, 0:n], bias_parts[:, q, :], own_block[:, :, 0:n], start=True, stop=False)
                for i in range(FQ):
                    f = q * FQ + i
                    for e in range(E2):
                        last = mm(blocks[:, i, 0:n], w1[:, e, f * 128:(f + 1) * 128],
                                  hnT[:, e, bass.ds(t * R, n)], start=False, stop=(i == FQ - 1 and e == E2 - 1))
                last.then_inc(y_psum, 1)

            def feed_forward_output(t, q, first=0, end=FQ):
                n = rows(t)
                if q == 0 and counts(t) and output_bank(t) is bank_z:
                    pe.wait_ge(res_ready, t)
                if not counts(t):
                    pe.wait_ge(dequant, 2 + q)
                pe.wait_ge(act_ready, 2 * t + q + 1)
                for f in range(q * FQ + first, q * FQ + end):
                    last = mm(output_bank(t)[0:n, 0:D], act2[:, f, 0:n], w2[:, f, :], start=(f == 0), stop=(f == FB - 1))
                if end == FQ:
                    last.then_inc(z_psum, 1)

            def slot(t, start=None, middle=None, end=None, normed=True, normed_last=False):
                if there(t - 1):
                    weigh(t - 1)
                if start:
                    start()
                if there(t - 2):
                    hidden(t - 2, 0)
                if middle:
                    middle()
                if there(t + 1):
                    values_and_paths(t + 1)
                if there(t - 1):
                    output_product(t - 1)
                if there(t - 2):
                    hidden(t - 2, 1)
                if there(t - 2):
                    feed_forward_output(t - 2, 0)
                if there(t - 2):
                    feed_forward_output(t - 2, 1, end=FQ if normed_last else FQ // 2)
                if end:
                    end()
                if there(t - 1) and normed:
                    turn_normed(t - 1)
                if there(t - 2) and not normed_last:
                    feed_forward_output(t - 2, 1, first=FQ // 2)

            turn_block(0, 0)
            turn_block(0, 1)
            pe.wait_ge(tok_par_in, 16 * N_TOK_PAR)
            for e in range(E2):
                pe.transpose(bank_o[:, e * T:(e + 1) * T], pos_rows[:, e * 128:(e + 1) * 128], ident[0:T, 0:T])
            pe.transpose(bank_o[:, E2 * T:E2 * T + N_VEC], tok_rows[:], ident[0:N_VEC, 0:N_VEC]).then_inc(pos_psum, 1)
            pe.wait_ge(wT_ready, 3)
            pe.wait_ge(xT_dve, 1)
            pe.wait_ge(xT_act, 1)
            project(0, 0, range(0, 2))
            turn_block(1, 0)
            turn_block(1, 1)
            project(0, 1, range(0, 2))
            turn_block(2, 0)
            turn_block(2, 1)
            pe.wait_ge(xT_dve, 2)
            pe.wait_ge(xT_act, 2)
            project(0, 0, range(2, 4))
            project(0, 1, range(2, 4))
            pe.wait_ge(xT_dve, 3)
            pe.wait_ge(xT_act, 3)
            project(0, 0, range(4, KT))
            project(0, 1, range(4, KT))
            turn_block(3, 0)
            turn_block(3, 1)
            pe.wait_ge(posb_step, E2)
            pe.wait_ge(par_in, 16 * N_PAR)
            pe.transpose(bank_o[:, 0:N_VEC], ln_rows[:], ident[0:N_VEC, 0:N_VEC])
            pe.wait_ge(by_depth, 1)
            pe.transpose(bank_o[0:HD, N_VEC:N_VEC + 1], bp_row_dh[:], ident[0:1, 0:1]).then_inc(par_psum, 1)
            pe.wait_ge(cls_ready, E2)
            project_paths(0)
            turn_block(4, 0)
            turn_block(4, 1)
            project(1, 0)
            pe.wait_ge(mats_in, 16 * N_MATS)
            pe.wait_ge(consts, N_CONST)
            slot(-1)
            turn_block(5, 0)
            turn_block(5, 1)
            project(1, 1)
            pe.wait_ge(xT_dve, 2 * C)
            pe.wait_ge(xT_act, 2 * C)
            project(2, 0)
            project_paths(1)
            slot(0)
            project(2, 1)

            def last_patches():
                project(3, 1)
                project_paths(2)

            slot(1, middle=lambda: project(3, 0), end=last_patches, normed=False)

            def normed_and_paths():
                turn_normed(0)
                project_paths(3)

            slot(2, start=normed_and_paths, normed_last=True)
            with pe.Fori(LOOP.start, LOOP.stop) as t:
                slot(t)
            slot(TILES - 2)
            slot(TILES - 1)
            t = TILES - 1
            weigh(t)
            hidden(t - 1, 0)
            output_product(t)
            hidden(t - 1, 1)
            feed_forward_output(t - 1, 0)
            feed_forward_output(t - 1, 1, end=FQ // 2)
            turn_normed(t)
            feed_forward_output(t - 1, 1, first=FQ // 2)
            hidden(t, 0)
            hidden(t, 1)
            feed_forward_output(t, 0)
            feed_forward_output(t, 1)

        @block.scalar
        def _(act):
            act.preload_act_table(ACT.Exp)
            for dst, src in (
                (pos_rows[:], pos.rearrange("o t d -> (o t) d")),
                (tok_rows[0:E2], tok_b.rearrange("(e p) -> e p", p=128)),
                (tok_rows[E2:N_VEC], cls_token.rearrange("o q (e p) -> (o q e) p", p=128)),
            ):
                act.dma_start(dst, src).then_inc(tok_par_in, 16)

            for j, bank in enumerate((bank_t, bank_z, bank_v)):
                act.wait_ge(wT_psum, j + 1)
                act.activation(wT[:, 2 * j:2 * j + 2, :], bank[:].rearrange("p (k d) -> p k d", k=2),
                               ACT.Copy).then_inc(wT_ready, 1)

            def x_columns(n):
                act.wait_ge(xT_psum, 2 * n + 2)
                half, c = divmod(n, C)
                dst = xT[:, 2 * c + 1, half * HR * GRID:(half + 1) * HR * GRID].rearrange("p (r a g) -> p a g r", a=2, g=3)
                src = bank_cd[:, :, 0:3 * HR].rearrange("p a (g r) -> p a g r", g=3)
                act.activation(dst, src, ACT.Copy).then_inc(xT_act, 1)

            def paths(c):
                cols = slice(c * CT, (c + 1) * CT)
                act.wait_ge(path_psum, c + 1)
                act.activation(path_f[:, cols], path_bank(c)[0:HD, 0:CT], ACT.Tanh, scale=0.5, bias=bp_half[:]).then_inc(path_f_ready, 1)
                act.wait_ge(path_f_ready, c + 1)
                act.activation(path_parts[:, 0, cols], path_f[:, cols], ACT.Copy, scale=0.5).then_inc(path_hi_ready, 1)

            def own_paths(t):
                n = rows(t)
                act.wait_ge(proj_done, t + 1)
                if counts(t):
                    act.wait_ge(u_done, t)
                act.activation(path_k[0:n, :], bank_v[0:n, D:D + HD], ACT.Copy).then_inc(path_k_ready, 1)

            def agreements(t):
                n = rows(t)
                act.wait_ge(u_done, t + 1)
                act.activation(agree[0:n, H:4 * H, :], agree[0:n, H:4 * H, :], ACT.Copy, bias=0.5).then_inc(g_done, 1)

            def values(t):
                n = rows(t)
                act.wait_ge(proj_done, t + 1)
                if counts(t):
                    act.wait_ge(pv_done, t)
                act.activation(v_rows[0:n, :], bank_v[0:n, 0:D], ACT.Copy).then_inc(v_ready, 1)

            def exponentials(t):
                n = rows(t)
                act.wait_ge(sim_ready, t + 1)
                if counts(t):
                    act.wait_ge(pv_done, t)
                for b in range(images(t)):
                    last = act.activation(probs[0:n, :, b, :], sim[0:n], ACT.Exp, scale=1.0 / DEPTH,
                                          bias=own_image[0:n, b:b + 1])
                last.then_inc(probs_ready, 1)

            def normed_columns(t):
                n = rows(t)
                act.wait_ge(n2T_psum, t + 1)
                for e in range(E2):
                    last = act.activation(hnT[:, e, bass.ds(t * R, n)], bank_turn[:, e * R:e * R + n], ACT.Identity,
                                          scale=gamma_col[:, e:e + 1], bias=beta_col[:, e:e + 1])
                last.then_inc(hnT_ready, 1)

            def half_tanh(t, q):
                n = rows(t)
                act.wait_ge(y_psum, 2 * t + q + 1)
                act.activation(th[:, q, :, 0:n], bank_y[:, q, 0:FQ * R].rearrange("p (f n) -> p f n", f=FQ)[:, :, 0:n],
                               ACT.Tanh, scale=0.5).then_inc(th_ready, 1)

            def slot(t, start=None, middle=None, end=None, early_values=False):
                if early_values:
                    values(t)
                if there(t):
                    agreements(t)
                if there(t) and not early_values:
                    values(t)
                if start:
                    start()
                if there(t - 2):
                    half_tanh(t - 2, 0)
                if there(t + 1):
                    own_paths(t + 1)
                if there(t - 2):
                    half_tanh(t - 2, 1)
                if middle:
                    middle()
                if there(t):
                    exponentials(t)
                if end:
                    end()
                if there(t - 1):
                    normed_columns(t - 1)

            for n in range(4):
                x_columns(n)
            act.wait_ge(colwise, 2)
            paths(0)
            x_columns(4)
            act.wait_ge(b2_in, 16)
            act.activation(b2_quarter[:], b2_quarter[:], ACT.Copy, scale=0.25).then_inc(b2_ready, 1)
            act.wait_ge(consts, N_CONST)
            slot(-1)
            x_columns(5)
            slot(0, start=lambda: paths(1), early_values=True)

            def second_scales():
                act.wait_ge(s2_in, 16)
                act.activation(s2[:], s2[:], ACT.Copy, scale=0.25).then_inc(s2_ready, 1)

            slot(1, middle=second_scales, end=lambda: paths(2))
            slot(2, start=lambda: paths(3))
            with act.Fori(LOOP.start, LOOP.stop) as t:
                slot(t)
            for t in range(LOOP.stop, TILES + 2):
                slot(t)

        @block.vector
        def _(dve):
            tt, ts, stt = dve.tensor_tensor, dve.tensor_scalar, dve.scalar_tensor_tensor
            def by_patch(n):
                dve.wait_ge(x_in[n], 16)
                if n >= 2:
                    dve.wait_ge(xT_psum, 2 * n - 2)
                dve.tensor_copy(x_pat[:, n % 2].rearrange("p g (i j) -> p g i j", i=PATCH),
                                x_rows[:, n, :].rearrange("p (i g j) -> p g i j", i=PATCH, g=GRID)).then_inc(x_pat_ready, 1)

            def x_columns(n):
                dve.wait_ge(xT_psum, 2 * n + 1)
                half, c = divmod(n, C)
                dst = xT[:, 2 * c, half * HR * GRID:(half + 1) * HR * GRID].rearrange("p (r a g) -> p a g r", a=2, g=3)
                src = bank_y[:, :, 0:3 * HR].rearrange("p a (g r) -> p a g r", g=3)
                dve.tensor_copy(dst, src).then_inc(xT_dve, 1)

            def tokens(c, e):
                dve.wait_ge(tok_psum, E2 * c + e + 1)
                tt(image_rows(hT[:, e, c * CT:(c + 1) * CT], T)[:, :, 1:T], image_rows((bank_t, bank_z)[e][:, 0:CP], NP),
                   spread(posb[:, e, 1:T], CI), ALU.add).then_inc(hT_ready, 1)

            def split_paths(c):
                cols = slice(c * CT, (c + 1) * CT)
                dve.wait_ge(path_hi_ready, c + 1)
                if c > 0:
                    dve.wait_ge(split_step, 3 * c)
                stt(out=path_rest[:], in0=path_f[:, cols], scalar=0.5, in1=path_parts[:, 0, cols], op0=ALU.mult,
                    op1=ALU.subtract).then_inc(split_step, 1)
                dve.wait_ge(split_step, 3 * c + 1)
                dve.tensor_copy(path_parts[:, 1, cols], path_rest[:]).then_inc(split_step, 1)
                dve.wait_ge(split_step, 3 * c + 2)
                tt(path_parts[:, 2, cols], path_rest[:], path_parts[:, 1, cols], ALU.subtract).then_inc(split_step, 1)

            def products(t):
                n = rows(t)
                dve.wait_ge(path_q_in, 16 * min((t + 1) * IT, B) if isinstance(t, int) else 16 * IT * (t + 1))
                dve.wait_ge(path_k_ready, t + 1)
                if counts(t):
                    dve.wait_ge(sim_ready, t)
                tt(agree[0:n], path_q[0:n, :].rearrange("p (r q) -> p r q", q=T),
                   path_k[0:n, :].rearrange("p (r o) -> p r o", o=1).broadcast_to([n, HD, T]),
                   ALU.mult).then_inc(u_done, 1)

            def depth(t, j):
                return agree[0:rows(t), j * H:(j + 1) * H, :].rearrange("p h q -> p (h q)")

            def inner_similarities(t):
                n = rows(t)
                dve.wait_ge(g_done, t + 1)
                stt(out=horner[0:n, 0, :], in0=depth(t, 0), scalar=1.5, in1=depth(t, 1), op0=ALU.add,
                    op1=ALU.mult).then_inc(horner_step, 1)
                dve.wait_ge(horner_step, 3 * t + 1)
                stt(out=horner[0:n, 1, :], in0=horner[0:n, 0, :], scalar=1.0, in1=depth(t, 2), op0=ALU.add,
                    op1=ALU.mult).then_inc(horner_step, 1)

            def outer_similarities(t):
                n = rows(t)
                dve.wait_ge(horner_step, 3 * t + 2)
                stt(out=horner[0:n, 0, :], in0=horner[0:n, 1, :], scalar=1.0, in1=depth(t, 3), op0=ALU.add,
                    op1=ALU.mult).then_inc(horner_step, 1)
                dve.wait_ge(g0_done, t + 1)
                dve.wait_ge(horner_step, 3 * t + 3)
                if counts(t):
                    dve.wait_ge(probs_ready, t)
                stt(out=sim[0:n].rearrange("p h q -> p (h q)"), in0=horner[0:n, 0, :], scalar=1.0, in1=depth(t, 4),
                    op0=ALU.add, op1=ALU.mult).then_inc(sim_ready, 1)

            def normalise_ctx(t):
                n = rows(t)
                dve.wait_ge(pv_done, t + 1)
                dve.reciprocal(recip[:, :, 0:n], weights[:, :, 0:n]).then_inc(recip_done, 1)
                dve.wait_ge(recip_done, t + 1)
                if counts(t):
                    dve.wait_ge(wo_done, t)
                tt(ctxT[:, :, 0:n], weighted[:, :, 0:n], recip[:, :, 0:n], ALU.mult).then_inc(ctxT_ready, 1)

            def measure(t):
                n = rows(t)
                dve.wait_ge(wo_done, t + 1)
                dve.bn_stats(stats[0:n, :], bank_o[0:n, 0:D])
                dve.drain()
                dve.bn_aggr(mv[0:n, :], stats[0:n, :]).then_inc(mv_ready, 1)

            def normalise(t):
                n = rows(t)
                dve.wait_ge(rstd_ready, t + 1)
                row = h2[0:n, bass.ds(t, 1), :].rearrange("p o d -> p (o d)")
                ts(row, bank_o[0:n, 0:D], mv[0:n, 0:1], rstd[0:n, 0:1], ALU.subtract, ALU.mult).then_inc(h2_ready, 1)
                dve.wait_ge(h2_ready, t + 1)
                if counts(t):
                    dve.wait_ge(n2T_psum, t)
                ts(n2[0:n, :], row, rstd[0:n, 1:2], None, ALU.mult).then_inc(n2_ready, 1)

            def silu(t, q):
                n = rows(t)
                dve.wait_ge(th_ready, 2 * t + q + 1)
                if counts(t):
                    dve.wait_ge(z_psum, 2 * t + q - 1)
                stt(out=act2[:, q * FQ:(q + 1) * FQ, 0:n], in0=th[:, q, :, 0:n], scalar=1.0,
                    in1=bank_y[:, q, 0:FQ * R].rearrange("p (f n) -> p f n", f=FQ)[:, :, 0:n], op0=ALU.add,
                    op1=ALU.mult).then_inc(act_ready, 1)

            def residual(t):
                n = rows(t)
                dve.wait_ge(z_psum, 2 * t + 2)
                dve.wait_ge(carry_ready, t + 1)
                if counts(t):
                    dve.wait_ge(fin_ready, t)
                row = h2[0:n, bass.ds(t, 1), :].rearrange("p o d -> p (o d)")
                stt(out=res[0:n, :], in0=row, scalar=2.0, in1=output_bank(t)[0:n, 0:D], op0=ALU.mult,
                    op1=ALU.add).then_inc(res_ready, 1)

            def measure_residual(t):
                n = rows(t)
                dve.wait_ge(res_ready, t + 1)
                dve.bn_stats(fstats[0:n, :], res[0:n, :])
                dve.drain()
                dve.bn_aggr(fmv[0:n, :], fstats[0:n, :]).then_inc(fmv_ready, 1)

            def final(t):
                n = rows(t)
                dve.wait_ge(frstd_ready, t + 1)
                if counts(t):
                    dve.wait_ge(stored, 16 * t)
                ts(fin[0:n, :], res[0:n, :], fmv[0:n, 0:1], frstd[0:n, 0:1], ALU.subtract, ALU.mult).then_inc(fin_ready, 1)

            def slot(t, middle=None, late=None, end=None, next_early=False):
                if there(t - 1):
                    normalise_ctx(t - 1)
                if there(t - 2):
                    silu(t - 2, 0)
                if there(t):
                    inner_similarities(t)
                if middle:
                    middle()
                if there(t - 3):
                    residual(t - 3)
                if there(t - 1):
                    measure(t - 1)
                if there(t):
                    outer_similarities(t)
                if there(t - 3):
                    measure_residual(t - 3)
                if there(t - 2):
                    silu(t - 2, 1)
                if late:
                    late()
                if next_early:
                    products(t + 1)
                if there(t - 1):
                    normalise(t - 1)
                if there(t - 3):
                    final(t - 3)
                if there(t + 1) and not next_early:
                    products(t + 1)
                if end:
                    end()

            by_patch(0)
            x_columns(0)
            by_patch(1)
            by_patch(2)
            dve.wait_ge(pos_psum, 1)
            dve.tensor_copy(tok_cols[:], bank_o[:, E2 * T:E2 * T + N_VEC]).then_inc(tok_cols_ready, 1)
            dve.wait_ge(tok_cols_ready, 1)
            for e in range(E2):
                ts(posb[:, e, 1:T], bank_o[:, e * T + 1:(e + 1) * T], tokb_col[:, e:e + 1], None, ALU.add)
                tt(posb[:, e, 0:1], bank_o[:, e * T:e * T + 1], cls_col[:, e:e + 1], ALU.add).then_inc(posb_step, 1)
            x_columns(1)
            dve.wait_ge(posb_step, E2)
            for e in range(E2):
                dve.tensor_copy(image_rows(hT[:, e, :], T)[:, :, 0], posb[:, e, 0:1].broadcast_to([128, B])).then_inc(cls_ready, 1)
            x_columns(2)
            by_patch(3)
            by_patch(4)
            dve.wait_ge(par_in, 16 * N_PAR)
            for j in range(DEPTH):
                d = DEPTH - 1 - j
                dve.tensor_copy(bp_row_dh[:, j * H:(j + 1) * H], bp_row[:].rearrange("o (h d) -> o h d", d=DEPTH)[:, :, d])
                last = dve.tensor_copy(wvp[:, :, D + j * H:D + (j + 1) * H],
                                       wp_dh[:].rearrange("p e (h d) -> p e h d", d=DEPTH)[:, :, :, d])
            last.then_inc(by_depth, 1)
            tokens(0, 0)
            tokens(0, 1)
            dve.wait_ge(par_psum, 1)
            dve.tensor_copy(ln_cols[:], bank_o[:, 0:N_VEC]).then_inc(colwise, 1)
            ts(bp_half[:], bank_o[0:HD, N_VEC:N_VEC + 1], 0.5, None, ALU.mult).then_inc(colwise, 1)
            x_columns(3)
            by_patch(5)
            split_paths(0)
            x_columns(4)
            dve.wait_ge(q1_in, 32)
            stt(out=w1[:], in0=q1[:], scalar=-ZERO_POINT, in1=s1[:], op0=ALU.add, op1=ALU.mult).then_inc(dequant, 1)
            tokens(1, 0)
            x_columns(5)
            tokens(1, 1)
            slot(-1)
            tokens(2, 0)

            slot(0, next_early=True)
            tokens(2, 1)
            split_paths(1)

            def second_weights(q):
                groups = slice(q * G2 // 2, (q + 1) * G2 // 2)
                stt(out=w2[:, groups, :], in0=q2[:, groups, :], scalar=-ZERO_POINT, in1=s2[:, groups, :], op0=ALU.add,
                    op1=ALU.mult).then_inc(dequant, 1)

            def last_tokens():
                tokens(3, 1)
                dve.wait_ge(q2_in, 16)
                dve.wait_ge(s2_ready, 1)
                second_weights(0)
                split_paths(2)

            slot(1, middle=lambda: tokens(3, 0), end=last_tokens, next_early=True)
            slot(2, middle=lambda: second_weights(1), late=lambda: split_paths(3))
            with dve.Fori(LOOP.start, LOOP.stop) as t:
                slot(t)
            for t in range(LOOP.stop, TILES + 3):
                slot(t)


_INS = ["x", "L0_tok_W", "L0_tok_b", "L0_tok_cls_token", "L0_tok_pos_embedding", "L0_attn_Wp", "L0_attn_bp",
        "L0_attn_Wv", "L0_attn_Wo", "L0_ffn_ln_gamma", "L0_ffn_ln_beta", "L0_ffn_fc1_q", "L0_ffn_fc1_scales",
        "L0_ffn_fc1_bias", "L0_ffn_fc2_q", "L0_ffn_fc2_scales", "L0_ffn_fc2_bias"]


def kernel(**inputs):
    import numpy as np
    import concourse.bacc as bacc
    from concourse.bass_utils import run_bass_kernel_spmd

    nc = bacc.Bacc("TRN2", target_bir_lowering=False, num_devices=1)
    arrays, args = {}, []
    for name in _INS:
        a = np.ascontiguousarray(inputs[name])
        arrays[f"in_{name}"] = a
        args.append(nc.dram_tensor(f"in_{name}", a.shape, mybir.dt.from_np(a.dtype), kind="ExternalInput").ap())
    B = inputs["x"].shape[0]
    _, T, D = inputs["L0_tok_pos_embedding"].shape
    args.append(nc.dram_tensor("out_0", (B, T, D), F32, kind="ExternalOutput").ap())
    vit_block(nc, *args)
    r = run_bass_kernel_spmd(nc, [arrays], core_ids=[0])
    return r.results[0]["out_0"]
```
